# Optimizing a Trainium2 kernel written in Bass

```python
import numpy as np
import jax
import jax.numpy as jnp

def _softmax(x, axis=-1):
    return jax.nn.softmax(x, axis=axis)

def _gelu(x):
    return jax.nn.gelu(x, approximate=True)

def _silu(x):
    return jax.nn.silu(x)

def _sigmoid(x):
    return jax.nn.sigmoid(x)

def _layernorm(x, axis=-1, eps=1e-05):
    m = jnp.mean(x, axis=axis, keepdims=True)
    v = jnp.var(x, axis=axis, keepdims=True)
    return (x - m) / jnp.sqrt(v + eps)

def _scatter_add(tgt, idx, src, axis=0):
    return tgt.at[idx].add(src)

def _segment_sum(src, seg, n):
    return jax.ops.segment_sum(src, seg, n)
kernel_name = 'mk_macaron_d1_jaxref_r8_ea59f0'

def setup_inputs(seed: int=0):
    np.random.seed(seed)
    _w = jnp.asarray

    def _L0_attn_setup():
        import jax, jax.numpy as jnp
        import numpy as np
        D_MODEL = 256
        D_INNER = 512
        D_XB = 128
        D_STATE = 16
        D_CONV = 4
        DT_RANK = 128
        INTER = 1024
        EPS = 1e-05
        H = D_INNER // D_STATE
        XB_HEADS = D_XB // D_STATE
        REP = D_INNER // D_XB
        GROUP = D_INNER // H
        BATCH, SEQ = (2, 128)

        def _rmsnorm(x, w):
            return x * jax.lax.rsqrt(jnp.mean(x * x, axis=-1, keepdims=True) + EPS) * w

        def _repeat_kv(x_heads):
            return jnp.repeat(x_heads, REP, axis=2)

        def _mamba_mixer(h, in_proj_w, conv_w, conv_b, dt_proj_w, dt_proj_b, A_log, D_param, out_proj_w):
            b, L, _ = h.shape
            zxbcdt = jnp.einsum('bld,pd->blp', h, in_proj_w)
            z, x, B, C, dt = jnp.split(zxbcdt, np.cumsum([D_INNER, D_XB, D_XB, D_INNER]), axis=-1)
            dt = jax.nn.softplus(jnp.einsum('blr,dr->bld', dt, dt_proj_w) + dt_proj_b)
            A = -jnp.exp(A_log)
            x = _repeat_kv(x.reshape(b, L, XB_HEADS, D_STATE)).reshape(b, L, D_INNER)
            Bh = _repeat_kv(B.reshape(b, L, XB_HEADS, D_STATE))
            Ch = C.reshape(b, L, H, D_STATE)
            xc = jax.lax.conv_general_dilated(x.transpose(0, 2, 1), conv_w, window_strides=(1,), padding=[(D_CONV - 1, 0)], feature_group_count=D_INNER, dimension_numbers=('NCH', 'OIH', 'NCH'))
            x = jax.nn.silu(xc + conv_b[None, :, None]).transpose(0, 2, 1)
            xT = x.transpose(1, 0, 2)
            dtT = dt.transpose(1, 0, 2)
            BT = Bh.transpose(1, 0, 2, 3)
            CT = Ch.transpose(1, 0, 2, 3)

            def step(hstate, inp):
                xt, dtt, Bt, Ct = inp
                dA = jnp.exp(dtt[..., None] * A)
                dBx = (dtt * xt).reshape(b, H, GROUP)[..., None] * Bt[:, :, None, :]
                hstate = dA * hstate + dBx.reshape(b, D_INNER, D_STATE)
                y = jnp.einsum('bhgn,bhn->bhg', hstate.reshape(b, H, GROUP, D_STATE), Ct)
                return (hstate, y.reshape(b, D_INNER))
            h0 = jnp.zeros((b, D_INNER, D_STATE), x.dtype)
            _, ys = jax.lax.scan(step, h0, (xT, dtT, BT, CT))
            y = ys.transpose(1, 0, 2) + x * D_param
            y = y * jax.nn.silu(z)
            return jnp.einsum('bld,md->blm', y, out_proj_w)
        key = jax.random.key(seed)
        ks = jax.random.split(key, 16)
        s = 0.02
        proj_dim = 2 * D_INNER + 2 * D_XB + DT_RANK
        dt = jnp.exp(jax.random.uniform(ks[0], (D_INNER,)) * (np.log(0.1) - np.log(0.001)) + np.log(0.001))
        dt = jnp.clip(dt, 0.0001)
        inv_dt = dt + jnp.log(-jnp.expm1(-dt))
        A = jnp.tile(jnp.arange(1, D_STATE + 1, dtype=jnp.float32)[None, :], (D_INNER, 1))
        return {'hidden_states': jax.random.normal(ks[1], (BATCH, SEQ, D_MODEL), jnp.float32), 'in_proj_w': jax.random.normal(ks[2], (proj_dim, D_MODEL), jnp.float32) * s, 'conv_w': jax.random.normal(ks[3], (D_INNER, 1, D_CONV), jnp.float32) * s, 'conv_b': jnp.zeros((D_INNER,), jnp.float32), 'dt_proj_w': jax.random.normal(ks[4], (D_INNER, DT_RANK), jnp.float32) * s, 'dt_proj_b': inv_dt, 'A_log': jnp.log(A), 'D_param': jnp.ones((D_INNER,), jnp.float32), 'out_proj_w': jax.random.normal(ks[5], (D_MODEL, D_INNER), jnp.float32) * s, 'ln1_w': jnp.ones((D_MODEL,), jnp.float32), 'ln2_w': jnp.ones((D_MODEL,), jnp.float32), 'gate_w': jax.random.normal(ks[6], (INTER, D_MODEL), jnp.float32) * s, 'up_w': jax.random.normal(ks[7], (INTER, D_MODEL), jnp.float32) * s, 'down_w': jax.random.normal(ks[8], (D_MODEL, INTER), jnp.float32) * s}
    _L0_attn_in = _L0_attn_setup()

    def _L0_ffn_setup():
        import jax, jax.numpy as jnp
        import numpy as np
        HID = 256
        N_EXP = 32
        F_EXP = 96
        TOP_K = 6
        F_SH = 192
        B, S = (1, 128)
        key = jax.random.key(seed)
        ks = jax.random.split(key, 8)
        s = 0.02
        return {'hidden_states': jax.random.normal(ks[0], (B, S, HID), dtype=jnp.float32), 'gate_w': jax.random.normal(ks[1], (HID, N_EXP), dtype=jnp.float32) * s, 'wg': jax.random.normal(ks[2], (N_EXP, HID, F_EXP), dtype=jnp.float32) * s, 'wu': jax.random.normal(ks[3], (N_EXP, HID, F_EXP), dtype=jnp.float32) * s, 'wd': jax.random.normal(ks[4], (N_EXP, F_EXP, HID), dtype=jnp.float32) * s, 'sg': jax.random.normal(ks[5], (HID, F_SH), dtype=jnp.float32) * s, 'su': jax.random.normal(ks[6], (HID, F_SH), dtype=jnp.float32) * s, 'sd': jax.random.normal(ks[7], (F_SH, HID), dtype=jnp.float32) * s}
    _L0_ffn_in = _L0_ffn_setup()
    _d = {'L0_attn_hidden_states': _L0_attn_in['hidden_states'], 'L0_attn_in_proj_w': _L0_attn_in['in_proj_w'], 'L0_attn_conv_w': _L0_attn_in['conv_w'], 'L0_attn_conv_b': _L0_attn_in['conv_b'], 'L0_attn_dt_proj_w': _L0_attn_in['dt_proj_w'], 'L0_attn_dt_proj_b': _L0_attn_in['dt_proj_b'], 'L0_attn_A_log': _L0_attn_in['A_log'], 'L0_attn_D_param': _L0_attn_in['D_param'], 'L0_attn_out_proj_w': _L0_attn_in['out_proj_w'], 'L0_attn_ln1_w': _L0_attn_in['ln1_w'], 'L0_attn_ln2_w': _L0_attn_in['ln2_w'], 'L0_attn_gate_w': _L0_attn_in['gate_w'], 'L0_attn_up_w': _L0_attn_in['up_w'], 'L0_attn_down_w': _L0_attn_in['down_w'], 'L0_ffn_gate_w': _L0_ffn_in['gate_w'], 'L0_ffn_wg': _L0_ffn_in['wg'], 'L0_ffn_wu': _L0_ffn_in['wu'], 'L0_ffn_wd': _L0_ffn_in['wd'], 'L0_ffn_sg': _L0_ffn_in['sg'], 'L0_ffn_su': _L0_ffn_in['su'], 'L0_ffn_sd': _L0_ffn_in['sd']}
    _x0 = _d['L0_attn_hidden_states']
    _d['L0_attn_hidden_states'] = jax.random.normal(jax.random.fold_in(jax.random.key(seed), 1), (8, 256, 256), dtype=_x0.dtype)
    del _x0
    return _d

def reference(L0_attn_hidden_states, L0_attn_in_proj_w, L0_attn_conv_w, L0_attn_conv_b, L0_attn_dt_proj_w, L0_attn_dt_proj_b, L0_attn_A_log, L0_attn_D_param, L0_attn_out_proj_w, L0_attn_ln1_w, L0_attn_ln2_w, L0_attn_gate_w, L0_attn_up_w, L0_attn_down_w, L0_ffn_gate_w, L0_ffn_wg, L0_ffn_wu, L0_ffn_wd, L0_ffn_sg, L0_ffn_su, L0_ffn_sd):

    def _L0_attn_ref(hidden_states, in_proj_w, conv_w, conv_b, dt_proj_w, dt_proj_b, A_log, D_param, out_proj_w, ln1_w, ln2_w, gate_w, up_w, down_w):
        import jax, jax.numpy as jnp
        import numpy as np
        D_MODEL = 256
        D_INNER = 512
        D_XB = 128
        D_STATE = 16
        D_CONV = 4
        DT_RANK = 128
        INTER = 1024
        EPS = 1e-05
        H = D_INNER // D_STATE
        XB_HEADS = D_XB // D_STATE
        REP = D_INNER // D_XB
        GROUP = D_INNER // H
        BATCH, SEQ = (2, 128)

        def _rmsnorm(x, w):
            return x * jax.lax.rsqrt(jnp.mean(x * x, axis=-1, keepdims=True) + EPS) * w

        def _repeat_kv(x_heads):
            return jnp.repeat(x_heads, REP, axis=2)

        def _mamba_mixer(h, in_proj_w, conv_w, conv_b, dt_proj_w, dt_proj_b, A_log, D_param, out_proj_w):
            b, L, _ = h.shape
            zxbcdt = jnp.einsum('bld,pd->blp', h, in_proj_w)
            z, x, B, C, dt = jnp.split(zxbcdt, np.cumsum([D_INNER, D_XB, D_XB, D_INNER]), axis=-1)
            dt = jax.nn.softplus(jnp.einsum('blr,dr->bld', dt, dt_proj_w) + dt_proj_b)
            A = -jnp.exp(A_log)
            x = _repeat_kv(x.reshape(b, L, XB_HEADS, D_STATE)).reshape(b, L, D_INNER)
            Bh = _repeat_kv(B.reshape(b, L, XB_HEADS, D_STATE))
            Ch = C.reshape(b, L, H, D_STATE)
            xc = jax.lax.conv_general_dilated(x.transpose(0, 2, 1), conv_w, window_strides=(1,), padding=[(D_CONV - 1, 0)], feature_group_count=D_INNER, dimension_numbers=('NCH', 'OIH', 'NCH'))
            x = jax.nn.silu(xc + conv_b[None, :, None]).transpose(0, 2, 1)
            xT = x.transpose(1, 0, 2)
            dtT = dt.transpose(1, 0, 2)
            BT = Bh.transpose(1, 0, 2, 3)
            CT = Ch.transpose(1, 0, 2, 3)

            def step(hstate, inp):
                xt, dtt, Bt, Ct = inp
                dA = jnp.exp(dtt[..., None] * A)
                dBx = (dtt * xt).reshape(b, H, GROUP)[..., None] * Bt[:, :, None, :]
                hstate = dA * hstate + dBx.reshape(b, D_INNER, D_STATE)
                y = jnp.einsum('bhgn,bhn->bhg', hstate.reshape(b, H, GROUP, D_STATE), Ct)
                return (hstate, y.reshape(b, D_INNER))
            h0 = jnp.zeros((b, D_INNER, D_STATE), x.dtype)
            _, ys = jax.lax.scan(step, h0, (xT, dtT, BT, CT))
            y = ys.transpose(1, 0, 2) + x * D_param
            y = y * jax.nn.silu(z)
            return jnp.einsum('bld,md->blm', y, out_proj_w)
        h = _rmsnorm(hidden_states, ln1_w)
        h = hidden_states + _mamba_mixer(h, in_proj_w, conv_w, conv_b, dt_proj_w, dt_proj_b, A_log, D_param, out_proj_w)
        h2 = _rmsnorm(h, ln2_w)
        mlp = jnp.einsum('bli,di->bld', jax.nn.silu(jnp.einsum('bld,id->bli', h2, gate_w)) * jnp.einsum('bld,id->bli', h2, up_w), down_w)
        return h + mlp

    def _L0_ffn_ref(hidden_states, gate_w, wg, wu, wd, sg, su, sd):
        import jax, jax.numpy as jnp
        import numpy as np
        HID = 256
        N_EXP = 32
        F_EXP = 96
        TOP_K = 6
        F_SH = 192
        B, S = (1, 128)
        orig_shape = hidden_states.shape
        x = hidden_states.reshape(-1, HID)
        scores = jax.nn.sigmoid(x @ gate_w)
        topk_w, topk_i = jax.lax.top_k(scores, TOP_K)
        topk_w = topk_w / (jnp.sum(topk_w, axis=-1, keepdims=True) + 1e-20)
        combine = jnp.sum(jax.nn.one_hot(topk_i, N_EXP, dtype=topk_w.dtype) * topk_w[..., None], axis=1)
        g = jnp.einsum('td,edf->tef', x, wg)
        u = jnp.einsum('td,edf->tef', x, wu)
        act = jax.nn.silu(g) * u
        routed = jnp.einsum('tef,efd,te->td', act, wd, combine)
        routed = routed.reshape(orig_shape)
        shared = jax.nn.silu(hidden_states @ sg) * (hidden_states @ su) @ sd
        return routed + shared
    x = L0_attn_hidden_states
    x = x + 0.5 * _L0_ffn_ref(_layernorm(x, axis=-1), L0_ffn_gate_w, L0_ffn_wg, L0_ffn_wu, L0_ffn_wd, L0_ffn_sg, L0_ffn_su, L0_ffn_sd)
    x = x + _L0_attn_ref(_layernorm(x, axis=-1), L0_attn_in_proj_w, L0_attn_conv_w, L0_attn_conv_b, L0_attn_dt_proj_w, L0_attn_dt_proj_b, L0_attn_A_log, L0_attn_D_param, L0_attn_out_proj_w, L0_attn_ln1_w, L0_attn_ln2_w, L0_attn_gate_w, L0_attn_up_w, L0_attn_down_w)
    x = x + 0.5 * _L0_ffn_ref(_layernorm(x, axis=-1), L0_ffn_gate_w, L0_ffn_wg, L0_ffn_wu, L0_ffn_wd, L0_ffn_sg, L0_ffn_su, L0_ffn_sd)
    return x

_drawn_inputs = setup_inputs


def setup_inputs(seed=0):
    import zlib

    import numpy as np

    out = dict(_drawn_inputs(seed))
    spreads = {'L0_attn_conv_b': (0.0, 0.8),
     'L0_attn_D_param': (1.0, 0.6),
     'L0_attn_ln1_w': (1.0, 0.6),
     'L0_attn_ln2_w': (1.0, 0.6)}
    factors = {'L0_attn_in_proj_w': 8.0,
     'L0_attn_conv_w': 8.0,
     'L0_attn_dt_proj_w': 8.0,
     'L0_attn_dt_proj_b': 8.0,
     'L0_attn_A_log': 8.0,
     'L0_attn_out_proj_w': 8.0,
     'L0_attn_gate_w': 3.026,
     'L0_attn_up_w': 2.982,
     'L0_attn_down_w': 2.981,
     'L0_ffn_gate_w': 8.0,
     'L0_ffn_wg': 8.0,
     'L0_ffn_wu': 8.0,
     'L0_ffn_wd': 8.0,
     'L0_ffn_sg': 5.223,
     'L0_ffn_su': 5.125,
     'L0_ffn_sd': 5.141}
    for name, (base, spread) in spreads.items():
        noise = np.random.default_rng([zlib.crc32(name.encode()), seed]).standard_normal(out[name].shape)
        drawn = base * np.exp(spread * noise) if base else spread * noise
        out[name] = jnp.asarray(drawn.astype(out[name].dtype))
    for name, factor in factors.items():
        out[name] = (out[name] * factor).astype(out[name].dtype)
    return out
```

```python
import concourse.bass as bass
from concourse import mybir
from contextlib import ExitStack

P = 128
SEQ, BATCH, DM = 256, 8, 256
KC = DM // P
EXPERTS, FEXP, TOPK, FSH = 32, 96, 6, 192
DI, NST, DXB, RANK, TAPS = 512, 16, 128, 128, 4
JC = DI // P
INTER = 1024
EPS = 1e-5
ROUTED = EXPERTS * FEXP // P
SHARED = 2
SHW = FSH // SHARED
FFN_CHUNKS = ROUTED + SHARED
MLP_CHUNKS = INTER // P
FH = EXPERTS * FEXP + FSH
PARTS = 3
TT = SEQ // P
PAIRS = NST // 2
UNITS = JC * PAIRS
SCW = EXPERTS + 2

GROWS = {
    "load": {"x_loaded": 16},
    "store": {"x2_free": 16},
    "gu": {"gu_filled": 1, "tanh_done": 1, "gated": 1, "hidden": 1},
    "cmb": {"comb_filled": 1, "weighted": 1},
    "down": {"down_done": 1},
    "end": {"residual": KC},
    "r0": {"r_base": 1},
    "n1c": {"side_filled": 1, "centered": 1, "squared": 1},
    "n1": {"squared": 1},
    "n2": {"side_filled": 1, "rooted": 1, "rstd": 1, "normed": KC},
    "rt1": {"side_filled": 1, "rt_exp": 1, "routing": 19},
    "rt2": {"side_filled": 1, "comb_ready": 1},
    "z": {"side_filled": 1, "z_tanh": 1, "z_done": 1},
    "x": {"side_filled": 1, "x_padded": 1, "conv": 2 * TAPS, "x_tanh": 1, "x_done": 1},
    "split": {"side_filled": 1, "part_hi": 2, "part_rest": 1, "part_mid": 1, "part_lo": 1,
              "stacked": 16 * 4 * PARTS},
    "dt": {"side_filled": 1, "dt_pre": 4, "dt_exp": 1},
    "sp": {"dt_ln": 1, "dt_fix": 4, "dtx": 1, "y_init": JC},
    "unit": {"b_filled": 1, "c_filled": 1, "decay": 2, "driven": 1, "scanned": 1, "read_out": 1,
             "y_sum": 2},
    "yz": {"y_gated": 1},
    "outp": {"side_filled": 1, "mixed": 2},
}


STARTS = {"x2_free": 16}


def kind_of(item):
    if item[0] == "n1" and item[1] in ("ln1", "lnA", "ln2"):
        return "n1c"
    return item[0]


def chunks_of(call):
    return MLP_CHUNKS if call == "mlp" else FFN_CHUNKS


def is_routed(call, c):
    return call != "mlp" and c < ROUTED


def items_of(mamba, post, first, nxt):
    if first:
        heavy = overlapped((["mlp"] if post else []) + ["f1"] + (["f2"] if post else []), nxt)
    else:
        heavy = overlapped(["mlp"], nxt) + overlapped(["f2"], nxt)
    before = []
    if first:
        before += [("n1", "ln1"), ("n2", "ln1"), ("rt1", "f1"), ("rt2", "f1")]
    light = []
    if mamba:
        light += [("n1", "lnA"), ("n2", "lnA"), ("n1", "rms1"), ("n2", "rms1")]
        light += [("split", 0), ("split", 1), ("split", 2), ("x", 0), ("x", 1), ("z", 0), ("z", 1)]
        light += [("dt", 0), ("dt", 1), ("sp",)]
        light += [("unit", u) for u in range(UNITS)]
        light += [("yz",), ("outp",), ("n1", "rms2"), ("n2", "rms2")]
    return merge(heavy, before, light, mamba, post)


def overlapped(calls, nxt):
    flat = [(call, c) for call in calls for c in range(chunks_of(call))]
    heavy = []
    for p in range(len(flat) + 2):
        if p < len(flat):
            heavy.append(("gu",) + flat[p])
        if 1 <= p <= len(flat) and is_routed(*flat[p - 1]):
            heavy.append(("cmb",) + flat[p - 1])
        if p >= 2:
            call, c = flat[p - 2]
            heavy.append(("down", call, c))
            if c == chunks_of(call) - 1:
                heavy.append(("end", call))
                if call == "f1" and nxt:
                    heavy.append(("load",))
                if call == "f2":
                    heavy.append(("store",))
    return heavy


def merge(heavy, before, light, mamba, post):
    if not post:
        out = list(before)
        rest = list(light)
        base = ("r0",) if mamba else None
        if mamba:
            n = 4
            out += rest[:4] + [base]
            rest = rest[4:]
        return out + spread(heavy, rest)
    cut = heavy.index(("end", "mlp")) + 1
    a, b = heavy[:cut], heavy[cut:]
    lead = before + light[:4]
    out = spread(a, lead)
    tail = ([("r0",)] if mamba else []) + [("n1", "ln2"), ("n2", "ln2"), ("rt1", "f2"), ("rt2", "f2")]
    if mamba:
        rest = light[4:]
        mixed = []
        for i in range(max(len(tail), 6)):
            mixed += tail[i:i + 1] + rest[i:i + 1]
        rest = mixed + rest[max(len(tail), 6):]
    else:
        rest = tail
    f2 = next(i for i, it in enumerate(b) if it[:2] == ("gu", "f2"))
    res = spread(b, rest)
    at = res.index(("gu", "f2", 0))
    need = res.index(("rt2", "f2"))
    if need > at:
        early = [it for it in rest[:rest.index(("rt2", "f2")) + 1]]
        late = rest[len(early):]
        res = spread(b[:f2], early) + spread(b[f2:], late)
    return out + res


def spread(heavy, light):
    out, done = [], 0
    for i, it in enumerate(heavy):
        out.append(it)
        upto = (i + 1) * len(light) // len(heavy)
        out += light[done:upto]
        done = upto
    return out + light[done:]


SIDE_FREED = {
    "n1c": [("centered", 1)], "n2": [("rooted", 1)], "rt1": [("rt_exp", 1)],
    "rt2": [("comb_ready", 1)], "z": [("z_done", 1)], "x": [("x_padded", 1)],
    "split": [("part_rest", 1)], "dt": [("dt_pre", 4)],
    "unit": [("driven", 1), ("read_out", 1)], "outp": [("mixed", 2)],
}


class Ledger:

    def __init__(self, steps, turns, loop_at):
        self.steps, self.loop_at = steps, loop_at
        self.before, self.base = [], []
        self.uses, self.use_base = [], []
        total, uses = dict(STARTS), 0
        for n, items in enumerate(steps):
            self.base.append(dict(total))
            local, at, mine = {}, {}, []
            for it in items:
                at[it] = dict(local)
                for s, k in GROWS[kind_of(it)].items():
                    local[s] = local.get(s, 0) + k
                for w, (s, k) in enumerate(SIDE_FREED.get(kind_of(it), [])):
                    mine.append((it, w, s, k))
            self.before.append(at)
            self.uses.append(mine)
            self.use_base.append(uses)
            times = turns if n == loop_at else 1
            if n == loop_at:
                self.per_turn = dict(local)
                assert len(mine) % 2 == 0
            for s, k in local.items():
                total[s] = total.get(s, 0) + k * times
            uses += len(mine) * times
        self.total = total


def macaron_kernel(nc, d):
    F32, BF16, I32 = mybir.dt.float32, mybir.dt.bfloat16, mybir.dt.int32
    ALU, ACT, AX = mybir.AluOpType, mybir.ActivationFunctionType, mybir.AxisListType

    steps = [
        [("load",)],
        items_of(False, False, True, True),
        items_of(True, False, True, True),
        items_of(True, True, True, True),
        items_of(True, True, True, False),
        items_of(True, True, False, False),
        items_of(False, True, False, False),
    ]
    LOOP = 3
    TURNS = BATCH - 3
    first_t = {0: -1, 1: 0, 2: 1, 3: 2, 4: BATCH - 1, 5: BATCH, 6: BATCH + 1}
    led = Ledger(steps, TURNS, LOOP)

    ctx = ExitStack()
    with ctx:
        def sb(name, shape, dt=F32):
            return ctx.enter_context(nc.sbuf_tensor(name, shape, dt))

        def bank(name):
            return ctx.enter_context(nc.psum_tensor(name, [P, 512], F32))

        w_gate = sb("w_gate", [P, KC, FH])
        w_up = sb("w_up", [P, KC, FH])
        w_down = sb("w_down", [P, FFN_CHUNKS, DM])
        w_router = sb("w_router", [P, KC, EXPERTS])
        PROJ = 2 * DI + DI + DXB + RANK
        w_in = sb("w_in", [P, KC, PROJ])
        w_dt = sb("w_dt", [P, DI])
        w_out = sb("w_out", [P, JC, DM])
        w_mgate = sb("w_mgate", [P, KC, INTER])
        w_mup = sb("w_mup", [P, KC, INTER])
        w_mdown = sb("w_mdown", [P, MLP_CHUNKS, DM])
        vecs = sb("vecs", [P, JC, 3 + TAPS])
        lnw = sb("lnw", [P, 2, KC])
        a_neg = sb("a_neg", [P, JC, NST])
        mean_w = sb("mean_w", [P, P])
        eps_col = sb("eps_col", [P, 1])
        marks = sb("marks", [P, TT, 2])
        ident = sb("ident", [P, P], BF16)
        sel_e = sb("sel_e", [PARTS * EXPERTS, ROUTED * P], BF16)
        sel_b = sb("sel_b", [PARTS * 32, NST * P], BF16)
        sel_c = sb("sel_c", [PARTS * 32, 4 * P], BF16)
        xin = sb("xin", [P, KC, SEQ])
        x1 = sb("x1", [P, KC, SEQ])
        hn = sb("hn", [P, KC, SEQ])
        res = sb("res", [P, KC, SEQ])
        x2 = sb("x2", [P, KC, SEQ])
        xn = {"f1": sb("xn_f1", [P, KC, SEQ]), "f2": sb("xn_f2", [P, KC, SEQ]),
              "mlp": sb("xn_mlp", [P, KC, SEQ])}
        comb = {"f1": sb("comb_f1", [PARTS * EXPERTS, SEQ], BF16),
                "f2": sb("comb_f2", [PARTS * EXPERTS, SEQ], BF16)}
        sq = sb("sq", [P, KC, SEQ])
        rstd = sb("rstd", [P, SEQ])
        hid = [sb(f"hid{i}", [P, SEQ]) for i in range(3)]
        z2 = sb("z2", [P, JC, SEQ])
        xs = sb("xs", [P, JC, SEQ])
        dts = sb("dts", [P, JC, SEQ])
        dtx = sb("dtx", [P, JC, SEQ])
        y = sb("y", [P, JC, SEQ])
        rn = y[:, 0:KC, :]
        xpad = sb("xpad", [P, 2, SEQ + TAPS - 1])
        tmp = sb("tmp", [P, 2, SEQ])
        parts = sb("parts", [P, PARTS, 2, SEQ], BF16)
        bst = sb("bst", [PARTS * 32, JC, SEQ], BF16)
        cst = sb("cst", [PARTS * 32, 4, JC, SEQ], BF16)
        ring = sb("ring", [P, 4, 2, SEQ])
        ubuf = ring[:, :, :, :].rearrange("p a b s -> p (a b) s")[:, 0:JC, :]
        lbuf = ring[:, :, :, :].rearrange("p a b s -> p (a b) s")[:, JC:2 * JC, :]
        dtr = ring[:, 3, 1, :]
        decay = [sb(f"decay{i}", [P, 2, SEQ]) for i in range(2)]
        sc = sb("sc", [P, TT, SCW])
        rep = sb("rep", [P, TT, SCW])
        top8 = sb("top8", [P, TT, 8])
        e_sc = sb("e_sc", [P, TT, EXPERTS])
        cm = sb("cm", [P, TT, EXPERTS])
        pace = sb("pace", [P, 1])
        csum = sb("csum", [P, TT])
        c3 = sb("c3", [P, TT, PARTS * EXPERTS], BF16)
        gub = [bank(f"gub{i}") for i in range(3)]
        cmb = bank("cmb")
        acc = [bank(f"acc{i}") for i in range(KC)]
        side = [bank(f"side{i}") for i in range(2)]

        names = sorted({s for g in GROWS.values() for s in g})
        sem = {s: ctx.enter_context(nc.semaphore(s)) for s in names}
        consts = ctx.enter_context(nc.semaphore("consts"))
        w_small = ctx.enter_context(nc.semaphore("w_small"))
        w_mamba = ctx.enter_context(nc.semaphore("w_mamba"))
        w_ffn = [ctx.enter_context(nc.semaphore(f"w_ffn{i}")) for i in range(4)]
        a_exp = ctx.enter_context(nc.semaphore("a_exp"))
        a_ready = ctx.enter_context(nc.semaphore("a_ready"))
        zeroed = ctx.enter_context(nc.semaphore("zeroed"))
        SLICES = [(0, 6), (6, 12), (12, 18), (18, ROUTED)]

        block = ctx.enter_context(nc.Block())

        class Step:

            def __init__(self, eng, n, turn):
                self.eng, self.n, self.turn = eng, n, turn
                self.at = led.before[n]

            def t(self):
                return first_t[self.n] if self.turn is None else self.turn + first_t[self.n]

            def value(self, s, v):
                if self.turn is None:
                    return v if v > 0 else None
                assert v > 0, s
                return self.turn * led.per_turn.get(s, 0) + v

            def count(self, s, item, k, back=0):
                return self.value(s, led.base[self.n].get(s, 0) + self.at[item].get(s, 0) + k - back)

            def prior(self, s):
                v = led.base[self.n].get(s, 0)
                return self.value(s, v) if v else None

            def side_of(self, item, w=0):
                return side[self.use(item, w) % 2]

            def use(self, item, w=0):
                local = next(i for i, u in enumerate(led.uses[self.n]) if u[0] == item and u[1] == w)
                return led.use_base[self.n] + local

            def side_use_before(self, item, w=0):
                mine = led.uses[self.n]
                local = self.use(item, w) - led.use_base[self.n]
                if local >= 2:
                    it, _, s, k = mine[local - 2]
                    return s, self.count(s, it, k)
                n = self.n - 1
                while n >= 0 and len(led.uses[n]) < 2:
                    n -= 1
                if n < 0:
                    return None
                s = led.uses[n][local - 2][2]
                assert self.n != LOOP or s == mine[local - 2][2]
                return s, self.prior(s)

            def chunk_no(self, item):
                return led.base[self.n].get("gu_filled", 0) + self.at[("gu",) + item[1:]]["gu_filled"] \
                    if "gu_filled" in self.at[("gu",) + item[1:]] \
                    else led.base[self.n].get("gu_filled", 0)

        def walk(eng, do):
            for n, items in enumerate(steps):
                if n == LOOP:
                    with eng.Fori(0, TURNS) as turn:
                        s = Step(eng, n, turn)
                        for it in items:
                            do(s, it)
                else:
                    s = Step(eng, n, None)
                    for it in items:
                        do(s, it)

        def pair(b):
            return b[:, :].rearrange("p (h s) -> p h s", h=2)

        def twice(ap):
            return ap.unsqueeze(1).broadcast_to([P, 2, SEQ])

        @block.sync
        def _(sp):
            for name, t in (("mean_w", mean_w), ("ident", ident), ("sel_e", sel_e),
                            ("sel_b", sel_b), ("sel_c", sel_c)):
                sp.dma_start(t[:], d[name]).then_inc(consts, 16)
            for name, t in (("w_router", w_router), ("vecs", vecs), ("lnw", lnw), ("a_log", a_neg)):
                sp.dma_start(t[:], d[name]).then_inc(w_small, 16)

            def ffn_slice(i):
                lo, hi = SLICES[i]
                a, b = lo * P, hi * P
                sp.dma_start(w_gate[:, :, a:b], d["w_gate"][:, :, a:b]).then_inc(w_ffn[i], 16)
                sp.dma_start(w_up[:, :, a:b], d["w_up"][:, :, a:b]).then_inc(w_ffn[i], 16)
                sp.dma_start(w_down[:, lo:hi, :], d["w_down"][:, lo:hi, :]).then_inc(w_ffn[i], 16)

            def do(s, it):
                if it[0] == "load":
                    if s.n > 0:
                        sp.wait_ge(sem["residual"], s.count("residual", ("end", "f1"), KC))
                    sp.dma_start(xin[:], d["x"][s.t() + 1]).then_inc(sem["x_loaded"], 16)
                    if s.n == 0:
                        for i in range(4):
                            ffn_slice(i)
                        sp.dma_start(w_gate[:, :, ROUTED * P:FH],
                                     d["w_gate"][:, :, ROUTED * P:FH]).then_inc(w_ffn[3], 16)
                        sp.dma_start(w_up[:, :, ROUTED * P:FH],
                                     d["w_up"][:, :, ROUTED * P:FH]).then_inc(w_ffn[3], 16)
                        sp.dma_start(w_down[0:SHW, ROUTED:FFN_CHUNKS, :],
                                     d["w_down_sh"]).then_inc(w_ffn[3], 16)
                        for name, t in (("w_in", w_in), ("w_dt", w_dt), ("w_out", w_out),
                                        ("w_mgate", w_mgate), ("w_mup", w_mup), ("w_mdown", w_mdown)):
                            sp.dma_start(t[:], d[name]).then_inc(w_mamba, 16)
                if it[0] == "split":
                    if it[1] == 0:
                        if (least := s.prior("c_filled")) is not None:
                            sp.wait_ge(sem["c_filled"], least)
                    sp.wait_ge(sem["part_lo"], s.count("part_lo", it, 1))
                    for q in range(4):
                        for a in range(PARTS):
                            rows = slice(32 * a, 32 * a + 32)
                            src = parts[32 * q:32 * q + 32, a, :, :]
                            if it[1] == 0:
                                dst, src = bst[rows, q, :], src[:, 0, :]
                            else:
                                j = 2 * (it[1] - 1)
                                dst = cst[rows, q, j:j + 2, :]
                            sp.dma_start(dst, src).then_inc(sem["stacked"], 16)
                if it[0] == "store":
                    sp.wait_ge(sem["residual"], s.count("residual", ("end", "f2"), KC))
                    sp.dma_start(d["out"][s.t() - 2], x2[:]).then_inc(sem["x2_free"], 16)

            walk(sp, do)
            sp.wait_ge(sem["x2_free"], STARTS["x2_free"] + 16 * BATCH)

        @block.tensor
        def _(pe):
            mm = nc.tensor.matmul
            pe.wait_ge(consts, 16 * 5)
            pe.wait_ge(w_small, 16 * 4)
            first_mamba = [True]

            def gu(s, it):
                _, call, c = it
                if c == 0:
                    norm = {"f1": "ln1", "f2": "ln2"}.get(call)
                    if norm:
                        pe.wait_ge(sem["normed"], s.count("normed", ("n2", norm), KC))
                    else:
                        pe.wait_ge(sem["normed"], s.prior("normed"))
                if s.n == 1:
                    for i, (lo, hi) in enumerate(SLICES):
                        if c == lo:
                            pe.wait_ge(w_ffn[i], 16 * (6 if i == 3 else 3))
                if (least := s.count("hidden", it, 1, back=3)) is not None:
                    pe.wait_ge(sem["hidden"], least)
                b = gub[s.chunk_no(it) % 3]
                wide = P if c < ROUTED else SHW
                lo = c * P if c < ROUTED else ROUTED * P + (c - ROUTED) * SHW
                g, u = (w_mgate, w_mup) if call == "mlp" else (w_gate, w_up)
                for half, w in ((0, g), (1, u)):
                    for k in range(KC):
                        last = mm(b[0:wide, half * SEQ:(half + 1) * SEQ], w[:, k, lo:lo + wide],
                                  xn[call][:, k, :], start=(k == 0), stop=(k == KC - 1))
                last.then_inc(sem["gu_filled"], 1)

            def do(s, it):
                kind = it[0]
                if kind == "gu":
                    gu(s, it)
                elif kind == "cmb":
                    _, call, c = it
                    if c == 0:
                        pe.wait_ge(sem["comb_ready"], s.count("comb_ready", ("rt2", call), 1))
                    if (least := s.count("weighted", it, 1, back=1)) is not None:
                        pe.wait_ge(sem["weighted"], least)
                    mm(cmb[:, 0:SEQ], sel_e[:, c * P:(c + 1) * P], comb[call][:, :],
                       start=True, stop=True).then_inc(sem["comb_filled"], 1)
                elif kind == "down":
                    _, call, c = it
                    if c == 0:
                        if (least := s.count("residual", ("end", call), 0)) is not None:
                            pe.wait_ge(sem["residual"], least)
                    if is_routed(call, c):
                        pe.wait_ge(sem["weighted"], s.count("weighted", ("cmb", call, c), 1))
                    else:
                        pe.wait_ge(sem["hidden"], s.count("hidden", ("gu", call, c), 1))
                    h = hid[s.chunk_no(it) % 3]
                    wide = P if (call == "mlp" or c < ROUTED) else SHW
                    w = w_mdown if call == "mlp" else w_down
                    for k in range(KC):
                        last = mm(acc[k][:, 0:SEQ], w[0:wide, c, k * P:(k + 1) * P], h[0:wide, :],
                                  start=(c == 0), stop=(c == chunks_of(call) - 1))
                    last.then_inc(sem["down_done"], 1)
                elif kind == "n1" and kind_of(it) == "n1c":
                    src = {"ln1": xin, "lnA": x1, "ln2": x2}[it[1]]
                    if it[1] == "ln1":
                        if (least := s.prior("x_loaded")) is not None:
                            pe.wait_ge(sem["x_loaded"], least)
                    elif it[1] == "lnA":
                        if (least := s.prior("residual")) is not None:
                            pe.wait_ge(sem["residual"], least)
                    else:
                        pe.wait_ge(sem["residual"], s.count("residual", ("end", "mlp"), KC))
                    if (last_use := s.side_use_before(it)) is not None:
                        pe.wait_ge(sem[last_use[0]], last_use[1])
                    for k in range(KC):
                        last = mm(s.side_of(it)[:, 0:SEQ], mean_w[:], src[:, k, :],
                                  start=(k == 0), stop=(k == KC - 1))
                    last.then_inc(sem["side_filled"], 1)
                elif kind == "n2":
                    pe.wait_ge(sem["squared"], s.count("squared", ("n1", it[1]), 1))
                    if (last_use := s.side_use_before(it)) is not None:
                        pe.wait_ge(sem[last_use[0]], last_use[1])
                    for k in range(KC):
                        last = mm(s.side_of(it)[:, 0:SEQ], mean_w[:], sq[:, k, :],
                                  start=(k == 0), stop=(k == KC - 1))
                    last.then_inc(sem["side_filled"], 1)
                elif kind == "rt1":
                    pe.wait_ge(sem["normed"], s.count("normed", ("n2", "ln1" if it[1] == "f1" else "ln2"), KC))
                    if (last_use := s.side_use_before(it)) is not None:
                        pe.wait_ge(sem[last_use[0]], last_use[1])
                    b = s.side_of(it)
                    for tt in range(TT):
                        for k in range(KC):
                            last = mm(b[:, tt * EXPERTS:(tt + 1) * EXPERTS],
                                      xn[it[1]][:, k, tt * P:(tt + 1) * P], w_router[:, k, :],
                                      start=(k == 0), stop=(k == KC - 1))
                    last.then_inc(sem["side_filled"], 1)
                elif kind == "rt2":
                    pe.wait_ge(sem["routing"], s.count("routing", ("rt1", it[1]), 19))
                    if (last_use := s.side_use_before(it)) is not None:
                        pe.wait_ge(sem[last_use[0]], last_use[1])
                    b = s.side_of(it)[:, :].bitcast(BF16)
                    for tt in range(TT):
                        last = nc.tensor.transpose(b[0:PARTS * EXPERTS, tt * P:(tt + 1) * P],
                                                   c3[:, tt, :], ident[:])
                    last.then_inc(sem["side_filled"], 1)
                elif kind in ("z", "x", "split"):
                    if kind == "split" and it[1] == 0:
                        pe.wait_ge(sem["normed"], s.count("normed", ("n2", "rms1"), KC))
                        if first_mamba[0]:
                            pe.wait_ge(w_mamba, 16 * 6)
                            first_mamba[0] = False
                    if (last_use := s.side_use_before(it)) is not None:
                        pe.wait_ge(sem[last_use[0]], last_use[1])
                    b = s.side_of(it)
                    at = {"z": 2 * it[1] * P, "x": DI + 2 * it[1] * P,
                          "split": 2 * DI + 2 * it[1] * P}[kind]
                    for h in range(2):
                        for k in range(KC):
                            last = mm(b[:, h * SEQ:(h + 1) * SEQ],
                                      w_in[:, k, at + h * P:at + (h + 1) * P], rn[:, k, :],
                                      start=(k == 0), stop=(k == KC - 1))
                    last.then_inc(sem["side_filled"], 1)
                elif kind == "dt":
                    pe.wait_ge(sem["part_hi"], s.count("part_hi", ("split", 0), 2))
                    if (last_use := s.side_use_before(it)) is not None:
                        pe.wait_ge(sem[last_use[0]], last_use[1])
                    b = s.side_of(it)
                    for h in range(2):
                        j = 2 * it[1] + h
                        last = mm(b[:, h * SEQ:(h + 1) * SEQ], w_dt[:, j * P:(j + 1) * P], dtr,
                                  start=True, stop=True)
                    last.then_inc(sem["side_filled"], 1)
                elif kind == "unit":
                    u = it[1]
                    j, p = u // PAIRS, u % PAIRS
                    if u == 0:
                        pe.wait_ge(sem["stacked"], s.count("stacked", ("split", 2), 16 * 4 * PARTS))
                    if (last_use := s.side_use_before(it, 0)) is not None:
                        pe.wait_ge(sem[last_use[0]], last_use[1])
                    b = s.side_of(it, 0)
                    for h in range(2):
                        n = 2 * p + h
                        last = mm(b[:, h * SEQ:(h + 1) * SEQ], sel_b[:, n * P:(n + 1) * P],
                                  bst[:, j, :], start=True, stop=True)
                    last.then_inc(sem["b_filled"], 1)
                    if (last_use := s.side_use_before(it, 1)) is not None:
                        pe.wait_ge(sem[last_use[0]], last_use[1])
                    b = s.side_of(it, 1)
                    for h in range(2):
                        n = 2 * p + h
                        last = mm(b[:, h * SEQ:(h + 1) * SEQ], sel_c[:, (n % 4) * P:(n % 4 + 1) * P],
                                  cst[:, n // 4, j, :], start=True, stop=True)
                    last.then_inc(sem["c_filled"], 1)
                elif kind == "outp":
                    pe.wait_ge(sem["y_gated"], s.count("y_gated", ("yz",), 1))
                    if (last_use := s.side_use_before(it)) is not None:
                        pe.wait_ge(sem[last_use[0]], last_use[1])
                    b = s.side_of(it)
                    for k in range(KC):
                        for j in range(JC):
                            last = mm(b[:, k * SEQ:(k + 1) * SEQ], w_out[:, j, k * P:(k + 1) * P],
                                      y[:, j, :], start=(j == 0), stop=(j == JC - 1))
                    last.then_inc(sem["side_filled"], 1)

            walk(pe, do)

        @block.scalar
        def _(act):
            A = nc.scalar.activation
            act.wait_ge(w_small, 16 * 4)
            A(a_neg[:], a_neg[:], ACT.Exp).then_inc(a_exp, 1)
            act.wait_ge(zeroed, 6)

            def do(s, it):
                kind = it[0]
                if kind == "gu":
                    _, call, c = it
                    wide = P if (call == "mlp" or c < ROUTED) else SHW
                    i = s.chunk_no(it)
                    act.wait_ge(sem["gu_filled"], s.count("gu_filled", it, 1))
                    if (least := s.count("down_done", ("down", call, c), 1, back=3)) is not None:
                        act.wait_ge(sem["down_done"], least)
                    A(hid[i % 3][0:wide, :], gub[i % 3][0:wide, 0:SEQ], ACT.Tanh,
                      scale=0.5).then_inc(sem["tanh_done"], 1)
                elif kind == "n1":
                    src = {"ln1": xn["f1"], "ln2": xn["f2"], "lnA": hn, "rms1": hn, "rms2": hn}[it[1]]
                    if kind_of(it) == "n1c":
                        act.wait_ge(sem["centered"], s.count("centered", it, 1))
                    elif it[1] == "rms1":
                        act.wait_ge(sem["normed"], s.count("normed", ("n2", "lnA"), KC))
                    else:
                        act.wait_ge(sem["mixed"], s.count("mixed", ("outp",), 1))
                    A(sq[:], src[:], ACT.Square).then_inc(sem["squared"], 1)
                elif kind == "n2":
                    act.wait_ge(sem["side_filled"], s.count("side_filled", it, 1))
                    A(rstd[:], s.side_of(it)[:, 0:SEQ], ACT.Sqrt,
                      bias=eps_col[:, 0:1]).then_inc(sem["rooted"], 1)
                elif kind == "rt1":
                    act.wait_ge(sem["side_filled"], s.count("side_filled", it, 1))
                    A(e_sc[:], s.side_of(it)[:, 0:TT * EXPERTS].rearrange("p (a e) -> p a e", a=TT),
                      ACT.Exp, scale=-1.0).then_inc(sem["rt_exp"], 1)
                elif kind == "z":
                    act.wait_ge(sem["side_filled"], s.count("side_filled", it, 1))
                    j = 2 * it[1]
                    if j == 0:
                        if (least := s.prior("y_gated")) is not None:
                            act.wait_ge(sem["y_gated"], least)
                    A(z2[:, j:j + 2, :], pair(s.side_of(it)), ACT.Tanh,
                      scale=0.5).then_inc(sem["z_tanh"], 1)
                elif kind == "x":
                    act.wait_ge(sem["side_filled"], s.count("side_filled", it, 1))
                    if (least := s.count("conv", it, 0)) is not None:
                        act.wait_ge(sem["conv"], least)
                    A(xpad[:, :, TAPS - 1:], pair(s.side_of(it)), ACT.Copy).then_inc(sem["x_padded"], 1)
                    act.wait_ge(sem["conv"], s.count("conv", it, 2 * TAPS))
                    act.wait_ge(sem["part_lo"], s.count("part_lo", ("split", 2), 1))
                    if (least := s.count("x_done", it, 0)) is not None:
                        act.wait_ge(sem["x_done"], least)
                    A(tmp[:], xs[:, 2 * it[1]:2 * it[1] + 2, :], ACT.Tanh).then_inc(sem["x_tanh"], 1)
                elif kind == "split":
                    act.wait_ge(sem["side_filled"], s.count("side_filled", it, 1))
                    if (least := s.count("stacked", it, 0)) is not None:
                        act.wait_ge(sem["stacked"], least)
                    b = pair(s.side_of(it))
                    if it[1] == 0:
                        A(dtr, b[:, 1, :], ACT.Copy).then_inc(sem["part_hi"], 1)
                        A(parts[:, 0, 0, :], b[:, 0, :], ACT.Copy).then_inc(sem["part_hi"], 1)
                        act.wait_ge(sem["part_rest"], s.count("part_rest", it, 1))
                        A(parts[:, 1, 0, :], tmp[:, 0, :], ACT.Copy).then_inc(sem["part_mid"], 1)
                    else:
                        for h in range(2):
                            A(parts[:, 0, h, :], b[:, h, :], ACT.Copy).then_inc(sem["part_hi"], 1)
                        act.wait_ge(sem["part_rest"], s.count("part_rest", it, 1))
                        A(parts[:, 1, :, :], tmp[:], ACT.Copy).then_inc(sem["part_mid"], 1)
                elif kind == "dt":
                    act.wait_ge(sem["side_filled"], s.count("side_filled", it, 1))
                    if it[1] == 0:
                        if (least := s.prior("y_sum")) is not None:
                            act.wait_ge(sem["y_sum"], least)
                        if (least := s.prior("decay")) is not None:
                            act.wait_ge(sem["decay"], least)
                    b = pair(s.side_of(it))
                    for h in range(2):
                        j = 2 * it[1] + h
                        A(ubuf[:, j, :], b[:, h, :], ACT.Abs, bias=vecs[:, j, 1:2]).then_inc(sem["dt_pre"], 1)
                        A(dts[:, j, :], b[:, h, :], ACT.Relu, bias=vecs[:, j, 1:2]).then_inc(sem["dt_pre"], 1)
                    act.wait_ge(sem["dt_pre"], s.count("dt_pre", it, 4))
                    u = ubuf[:, 2 * it[1]:2 * it[1] + 2, :]
                    A(u, u, ACT.Exp, scale=-1.0).then_inc(sem["dt_exp"], 1)
                elif kind == "sp":
                    act.wait_ge(sem["dt_exp"], s.count("dt_exp", ("dt", 1), 1))
                    A(lbuf, ubuf, ACT.Ln, bias=1.0).then_inc(sem["dt_ln"], 1)
                elif kind == "unit":
                    u = it[1]
                    j, p = u // PAIRS, u % PAIRS
                    if u == 0:
                        act.wait_ge(sem["dt_fix"], s.count("dt_fix", ("sp",), 4))
                        if s.n == 2:
                            act.wait_ge(a_ready, 1)
                    if (least := s.count("scanned", it, 1, back=2)) is not None:
                        act.wait_ge(sem["scanned"], least)
                    for h in range(2):
                        n = 2 * p + h
                        A(decay[u % 2][:, h, 1:SEQ], dts[:, j, 1:SEQ], ACT.Exp,
                          scale=a_neg[:, j, n:n + 1]).then_inc(sem["decay"], 1)

            walk(act, do)

        @block.vector
        def _(dve):
            v = nc.vector
            v.memset(decay[0][:, :, 0:1], 0.0).then_inc(zeroed, 1)
            v.memset(decay[1][:, :, 0:1], 0.0).then_inc(zeroed, 1)
            v.memset(xpad[:, :, 0:TAPS - 1], 0.0).then_inc(zeroed, 1)
            v.memset(x2[:], 0.0).then_inc(sem["x2_free"], STARTS["x2_free"])
            v.memset(eps_col[:], EPS).then_inc(zeroed, 1)
            v.memset(marks[:, :, 0:1], -1.0).then_inc(zeroed, 1)
            v.memset(marks[:, :, 1:2], -2.0).then_inc(zeroed, 1)
            dve.wait_ge(zeroed, 6)
            dve.wait_ge(a_exp, 1)
            v.tensor_scalar(a_neg[:], a_neg[:], -1.0, None, ALU.mult).then_inc(a_ready, 1)
            v.tensor_copy(sc[:, :, EXPERTS:SCW], marks[:]).then_inc(a_ready, 1)
            v.tensor_scalar(vecs[:, :, 2:], vecs[:, :, 2:], 0.5, None, ALU.mult).then_inc(a_ready, 1)
            dve.wait_ge(a_ready, 3)

            def do(s, it):
                kind = it[0]
                if kind == "gu":
                    _, call, c = it
                    wide = P if (call == "mlp" or c < ROUTED) else SHW
                    i = s.chunk_no(it)
                    h, b = hid[i % 3][0:wide, :], gub[i % 3]
                    dve.wait_ge(sem["tanh_done"], s.count("tanh_done", it, 1))
                    v.scalar_tensor_tensor(h, h, 1.0, b[0:wide, 0:SEQ], ALU.add,
                                           ALU.mult).then_inc(sem["gated"], 1)
                    dve.wait_ge(sem["gated"], s.count("gated", it, 1))
                    v.tensor_tensor(h, h, b[0:wide, SEQ:2 * SEQ], ALU.mult).then_inc(sem["hidden"], 1)
                elif kind == "cmb":
                    _, call, c = it
                    h = hid[s.chunk_no(it) % 3]
                    dve.wait_ge(sem["comb_filled"], s.count("comb_filled", it, 1))
                    dve.wait_ge(sem["hidden"], s.count("hidden", ("gu", call, c), 1))
                    v.tensor_tensor(h[:], h[:], cmb[:, 0:SEQ], ALU.mult).then_inc(sem["weighted"], 1)
                elif kind == "end":
                    call = it[1]
                    dve.wait_ge(sem["down_done"], s.count("down_done", ("down", call, chunks_of(call) - 1), 1))
                    src, dst, scale = {"f1": (xin, x1, 0.25), "mlp": (res, x2, 0.5),
                                       "f2": (x2, x2, 0.25)}[call]
                    if call == "mlp":
                        if (least := s.prior("x2_free")) is not None:
                            dve.wait_ge(sem["x2_free"], least)
                    for k in range(KC):
                        v.scalar_tensor_tensor(dst[:, k, :], acc[k][:, 0:SEQ], scale, src[:, k, :],
                                               ALU.mult, ALU.add).then_inc(sem["residual"], 1)
                elif kind == "r0":
                    dve.wait_ge(sem["normed"], s.count("normed", ("n2", "lnA"), KC))
                    if ("end", "mlp") in s.at:
                        dve.wait_ge(sem["residual"], s.count("residual", ("end", "mlp"), KC))
                    v.tensor_tensor(res[:], x1[:], hn[:], ALU.add).then_inc(sem["r_base"], 1)
                elif kind == "n1":
                    if kind_of(it) == "n1c":
                        src, dst = {"ln1": (xin, xn["f1"]), "lnA": (x1, hn), "ln2": (x2, xn["f2"])}[it[1]]
                        dve.wait_ge(sem["side_filled"], s.count("side_filled", it, 1))
                        v.tensor_tensor(dst[:], src[:], twice(s.side_of(it)[:, 0:SEQ]),
                                        ALU.subtract).then_inc(sem["centered"], 1)
                elif kind == "n2":
                    dve.wait_ge(sem["rooted"], s.count("rooted", it, 1))
                    v.reciprocal(rstd[:], rstd[:]).then_inc(sem["rstd"], 1)
                    dve.wait_ge(sem["rstd"], s.count("rstd", it, 1))
                    for k in range(KC):
                        if it[1] in ("rms1", "rms2"):
                            dst = rn if it[1] == "rms1" else xn["mlp"]
                            i = 0 if it[1] == "rms1" else 1
                            v.scalar_tensor_tensor(dst[:, k, :], hn[:, k, :], lnw[:, i, k:k + 1], rstd[:],
                                                   ALU.mult, ALU.mult).then_inc(sem["normed"], 1)
                        else:
                            dst = {"ln1": xn["f1"], "lnA": hn, "ln2": xn["f2"]}[it[1]]
                            v.tensor_tensor(dst[:, k, :], dst[:, k, :], rstd[:],
                                            ALU.mult).then_inc(sem["normed"], 1)
                elif kind == "rt1":
                    route(s, it)
                elif kind == "rt2":
                    dve.wait_ge(sem["side_filled"], s.count("side_filled", it, 1))
                    v.tensor_copy(comb[it[1]][:], s.side_of(it)[:, :].bitcast(BF16)[0:PARTS * EXPERTS, 0:SEQ]
                                  ).then_inc(sem["comb_ready"], 1)
                elif kind == "z":
                    j = 2 * it[1]
                    dve.wait_ge(sem["z_tanh"], s.count("z_tanh", it, 1))
                    v.scalar_tensor_tensor(z2[:, j:j + 2, :], z2[:, j:j + 2, :], 1.0, pair(s.side_of(it)),
                                           ALU.add, ALU.mult).then_inc(sem["z_done"], 1)
                elif kind == "x":
                    dve.wait_ge(sem["x_padded"], s.count("x_padded", it, 1))
                    if it[1] == 0:
                        if (least := s.prior("y_init")) is not None:
                            dve.wait_ge(sem["y_init"], least)
                    for k in range(TAPS):
                        for h in range(2):
                            j = 2 * it[1] + h
                            o, i = xs[:, j, :], xpad[:, h, k:k + SEQ]
                            w = vecs[:, j, 3 + k:4 + k]
                            if k == 0:
                                v.tensor_scalar(o, i, w, vecs[:, j, 2:3], ALU.mult,
                                                ALU.add).then_inc(sem["conv"], 1)
                            else:
                                dve.wait_ge(sem["conv"], s.count("conv", it, 2 * k + h - 1))
                                v.scalar_tensor_tensor(o, i, w, o, ALU.mult,
                                                       ALU.add).then_inc(sem["conv"], 1)
                    dve.wait_ge(sem["x_tanh"], s.count("x_tanh", it, 1))
                    o = xs[:, 2 * it[1]:2 * it[1] + 2, :]
                    v.scalar_tensor_tensor(o, tmp[:], 1.0, o, ALU.add, ALU.mult).then_inc(sem["x_done"], 1)
                elif kind == "split":
                    dve.wait_ge(sem["part_hi"], s.count("part_hi", it, 2))
                    b = pair(s.side_of(it))
                    n = 1 if it[1] == 0 else 2
                    v.tensor_tensor(tmp[:, 0:n, :], b[:, 0:n, :], parts[:, 0, 0:n, :],
                                    ALU.subtract).then_inc(sem["part_rest"], 1)
                    dve.wait_ge(sem["part_mid"], s.count("part_mid", it, 1))
                    v.tensor_tensor(parts[:, 2, 0:n, :], tmp[:, 0:n, :], parts[:, 1, 0:n, :],
                                    ALU.subtract).then_inc(sem["part_lo"], 1)
                elif kind == "sp":
                    dve.wait_ge(sem["dt_exp"], s.count("dt_exp", ("dt", 1), 1))
                    if (least := s.prior("driven")) is not None:
                        dve.wait_ge(sem["driven"], least)
                    v.tensor_scalar(dtx[:], ubuf, 1.0, -1.0, ALU.add, ALU.add).then_inc(sem["dt_fix"], 1)
                    dve.wait_ge(sem["dt_fix"], s.count("dt_fix", it, 1))
                    v.tensor_tensor(dtx[:], ubuf, dtx[:], ALU.subtract).then_inc(sem["dt_fix"], 1)
                    dve.wait_ge(sem["dt_fix"], s.count("dt_fix", it, 2))
                    dve.wait_ge(sem["dt_ln"], s.count("dt_ln", it, 1))
                    v.tensor_tensor(dtx[:], dtx[:], lbuf, ALU.add).then_inc(sem["dt_fix"], 1)
                    dve.wait_ge(sem["dt_fix"], s.count("dt_fix", it, 3))
                    v.tensor_tensor(dts[:], dtx[:], dts[:], ALU.add).then_inc(sem["dt_fix"], 1)
                    dve.wait_ge(sem["dt_fix"], s.count("dt_fix", it, 4))
                    dve.wait_ge(sem["x_done"], s.count("x_done", ("x", 1), 1))
                    v.tensor_tensor(dtx[:], dts[:], xs[:], ALU.mult).then_inc(sem["dtx"], 1)
                    dve.wait_ge(sem["side_filled"], s.count("side_filled", ("z", 1), 1))
                    for j in range(JC):
                        v.tensor_scalar(y[:, j, :], xs[:, j, :], vecs[:, j, 0:1], None,
                                        ALU.mult).then_inc(sem["y_init"], 1)
                elif kind == "unit":
                    u = it[1]
                    j = u // PAIRS
                    w = ring[:, u % 3, :, :]
                    if u == 0:
                        dve.wait_ge(sem["dtx"], s.count("dtx", ("sp",), 1))
                    if u >= 3:
                        dve.wait_ge(sem["y_sum"], s.count("y_sum", ("unit", u - 3), 2))
                    dve.wait_ge(sem["b_filled"], s.count("b_filled", it, 1))
                    v.tensor_tensor(w, twice(dtx[:, j, :]), pair(s.side_of(it, 0)),
                                    ALU.mult).then_inc(sem["driven"], 1)
                    dve.wait_ge(sem["decay"], s.count("decay", it, 2))
                    dve.wait_ge(sem["driven"], s.count("driven", it, 1))
                    wf = w.rearrange("p h s -> p (h s)")
                    v.tensor_tensor_scan(wf, decay[u % 2][:, :, :].rearrange("p h s -> p (h s)"), wf,
                                         0.0, ALU.mult, ALU.add).then_inc(sem["scanned"], 1)
                    dve.wait_ge(sem["c_filled"], s.count("c_filled", it, 1))
                    dve.wait_ge(sem["scanned"], s.count("scanned", it, 1))
                    v.tensor_tensor(w, w, pair(s.side_of(it, 1)), ALU.mult).then_inc(sem["read_out"], 1)
                elif kind == "yz":
                    dve.wait_ge(sem["y_sum"], s.count("y_sum", ("unit", UNITS - 1), 2))
                    dve.wait_ge(sem["z_done"], s.count("z_done", ("z", 1), 1))
                    v.tensor_tensor(y[:], y[:], z2[:], ALU.mult).then_inc(sem["y_gated"], 1)
                elif kind == "outp":
                    dve.wait_ge(sem["side_filled"], s.count("side_filled", it, 1))
                    dve.wait_ge(sem["r_base"], s.count("r_base", ("r0",), 1))
                    b = pair(s.side_of(it))
                    v.scalar_tensor_tensor(hn[:], b, 0.5, hn[:], ALU.mult, ALU.add).then_inc(sem["mixed"], 1)
                    v.scalar_tensor_tensor(res[:], b, 0.5, res[:], ALU.mult, ALU.add).then_inc(sem["mixed"], 1)

            def route(s, it):
                done = [0]

                def link(ins):
                    done[0] += 1
                    ins.then_inc(sem["routing"], 1)

                def settle():
                    dve.wait_ge(sem["routing"], s.count("routing", it, done[0]))

                dve.wait_ge(sem["rt_exp"], s.count("rt_exp", it, 1))
                link(v.tensor_scalar(e_sc[:], e_sc[:], 1.0, None, ALU.add))
                settle()
                link(v.reciprocal(sc[:, :, 0:EXPERTS], e_sc[:]))
                settle()
                link(v.memset(pace[:], 0.0))
                for tt in range(TT):
                    link(v.max(top8[:, tt, :], sc[:, tt, 0:EXPERTS]))
                settle()
                link(v.tensor_copy(top8[:, :, TOPK:8], marks[:]))
                settle()
                link(v.memset(pace[:], 0.0))
                for tt in range(TT):
                    link(v.match_replace(rep[:, tt, :], top8[:, tt, :], sc[:, tt, :], 0.0))
                settle()
                link(v.tensor_tensor(cm[:], sc[:, :, 0:EXPERTS], rep[:, :, 0:EXPERTS], ALU.subtract))
                settle()
                link(v.tensor_reduce(csum[:], cm[:], axis=AX.X, op=ALU.add))
                settle()
                link(v.tensor_scalar(csum[:], csum[:], 1e-20, None, ALU.add))
                settle()
                link(v.reciprocal(csum[:], csum[:]))
                settle()
                for tt in range(TT):
                    link(v.tensor_scalar(cm[:, tt, :], cm[:, tt, :], csum[:, tt:tt + 1], None, ALU.mult))
                settle()
                E = EXPERTS
                link(v.tensor_copy(c3[:, :, 0:E], cm[:]))
                settle()
                link(v.tensor_tensor(cm[:], cm[:], c3[:, :, 0:E], ALU.subtract))
                settle()
                link(v.tensor_copy(c3[:, :, E:2 * E], cm[:]))
                settle()
                link(v.tensor_tensor(c3[:, :, 2 * E:3 * E], cm[:], c3[:, :, E:2 * E], ALU.subtract))
                assert done[0] == 19

            walk(dve, do)

        @block.gpsimd
        def _(pool):
            def do(s, it):
                if it[0] == "unit":
                    u = it[1]
                    j = u // PAIRS
                    if u == 0:
                        pool.wait_ge(sem["y_init"], s.count("y_init", ("sp",), JC))
                    pool.wait_ge(sem["read_out"], s.count("read_out", it, 1))
                    for h in range(2):
                        if u or h:
                            if (least := s.count("y_sum", it, h)) is not None:
                                pool.wait_ge(sem["y_sum"], least)
                        nc.gpsimd.tensor_tensor(y[:, j, :], y[:, j, :], ring[:, u % 3, h, :],
                                                ALU.add).then_inc(sem["y_sum"], 1)

            walk(pool, do)


def kernel(**inputs):
    import numpy as np
    import concourse.bacc as bacc
    from concourse import mybir as _m
    from concourse.bass_utils import run_bass_kernel_spmd as run
    import ml_dtypes

    g = {k.removeprefix("L0_"): np.asarray(v) for k, v in inputs.items()}
    c = np.ascontiguousarray

    def feat(a):
        return c(a.reshape(a.shape[0] // P, P, a.shape[1]).transpose(1, 0, 2))

    x = g["attn_hidden_states"]
    xt = c(x.reshape(BATCH, SEQ, KC, P).transpose(0, 3, 2, 1))
    gate = np.concatenate([g["ffn_wg"].transpose(1, 0, 2).reshape(DM, -1), g["ffn_sg"]], axis=1)
    up = np.concatenate([g["ffn_wu"].transpose(1, 0, 2).reshape(DM, -1), g["ffn_su"]], axis=1)
    down = feat(g["ffn_wd"].reshape(EXPERTS * FEXP, DM))
    down_sh = c(g["ffn_sd"].reshape(SHARED, SHW, DM).transpose(1, 0, 2))
    win = g["attn_in_proj_w"]
    zr = np.arange(DI)
    heads = DXB // NST
    rep = DI // DXB
    ch = np.arange(DI)
    xr = DI + (ch // (rep * NST)) * NST + ch % NST
    br = DI + DXB + np.arange(DXB)
    dr = 2 * DXB + 2 * DI + np.arange(RANK)
    q, hd, n4 = np.meshgrid(np.arange(4), np.arange(heads), np.arange(4), indexing="ij")
    cr = np.concatenate([(DI + 2 * DXB + (8 * j + hd) * NST + 4 * q + n4).ravel() for j in range(JC)])
    order = np.concatenate([zr, xr, br, dr, cr])
    w_in = feat(c(win[order].T))
    vecs = np.concatenate([g["attn_D_param"][:, None], g["attn_dt_proj_b"][:, None],
                           g["attn_conv_b"][:, None], g["attn_conv_w"][:, 0, :]], axis=1)
    lnw = np.stack([g["attn_ln1_w"], g["attn_ln2_w"]])
    bf = ml_dtypes.bfloat16
    m = np.arange(P)
    k96 = np.arange(PARTS * 32)[:, None] % 32
    f = np.arange(ROUTED * P)[None, :]
    sel_e = (k96 == f // FEXP).astype(bf)
    sel_b = np.concatenate([(k96 == (m[None] // 64) * NST + n) for n in range(NST)], 1).astype(bf)
    sel_c = np.concatenate([(k96 == (m[None] // NST) * 4 + n) for n in range(4)], 1).astype(bf)
    arrays = {
        "x": xt, "w_gate": feat(gate), "w_up": feat(up), "w_down": down, "w_down_sh": down_sh,
        "w_router": feat(g["ffn_gate_w"]), "w_in": w_in, "w_dt": c(g["attn_dt_proj_w"].T),
        "w_out": feat(c(g["attn_out_proj_w"].T)), "w_mgate": feat(c(g["attn_gate_w"].T)),
        "w_mup": feat(c(g["attn_up_w"].T)), "w_mdown": feat(c(g["attn_down_w"].T)),
        "vecs": feat(vecs), "lnw": c(lnw.reshape(2, KC, P).transpose(2, 0, 1)),
        "a_log": feat(g["attn_A_log"]),
        "mean_w": np.full((P, P), 1.0 / DM, np.float32), "ident": np.eye(P).astype(bf),
        "sel_e": sel_e, "sel_b": sel_b, "sel_c": sel_c,
    }
    arrays = {k: c(v) for k, v in arrays.items()}
    nc = bacc.Bacc("TRN2", target_bir_lowering=False, num_devices=1)
    d = {k: nc.dram_tensor(f"in_{k}", v.shape, _m.dt.from_np(v.dtype), kind="ExternalInput").ap()
         for k, v in arrays.items()}
    d["out"] = nc.dram_tensor("out", xt.shape, _m.dt.float32, kind="ExternalOutput").ap()
    macaron_kernel(nc, d)
    r = run(nc, [{f"in_{k}": v for k, v in arrays.items()}], core_ids=[0])
    y = np.asarray(r.results[0]["out"])
    return c(y.transpose(0, 3, 2, 1)).reshape(BATCH, SEQ, DM)
```

```python
import concourse.bass as bass
from concourse import mybir
from contextlib import ExitStack

P = 128
SEQ, BATCH, DM = 256, 8, 256
KC = DM // P
EXPERTS, FEXP, TOPK, FSH = 32, 96, 6, 192
DI, NST, DXB, RANK, TAPS = 512, 16, 128, 128, 4
JC = DI // P
INTER = 1024
EPS = 1e-5
ROUTED = EXPERTS * FEXP // P
FFN_CHUNKS = ROUTED + -(-FSH // P)
MLP_CHUNKS = INTER // P
PARTS = 3
TT = SEQ // P
PAIRS = NST // 2
UNITS = JC * PAIRS
SCW = EXPERTS + 2
WSLOTS, MSLOTS, HSLOTS = 3, 3, 3
SIDES, GUBS = 2, 3

GROWS = {
    "load": {"x_loaded": 16},
    "store": {"x2_free": 16},
    **{f"mg{i}": {"load_paced": 1, f"mlp_gu{i}": 16} for i in range(MSLOTS)},
    **{f"md{i}": {"load_paced": 1, f"mlp_down{i}": 16} for i in range(MSLOTS)},
    "again": {"x_again": 16},
    "hx": {"x_hi": 1, "x_split": 1},
    "keep": {"kept": 1},
    "ws": {"w_hi": 1, "w_split": 1},
    "g": {"g_filled": 1, "tanh_done": 1},
    "by_g": {"gated": 1},
    "u": {"u_filled": 1},
    "by_u": {"hidden": 1},
    "gum": {"m_filled": 1, "tanh_done": 1, "gated": 1, "hidden": 1},
    "cmb": {"comb_filled": 1},
    "by_comb": {"weighted": 1},
    "down": {"down_done": 1},
    "end": {"residual": KC},
    "r0": {"r_base": 1},
    "n1c": {"side_filled": 1, "centered": 1, "squared": 1},
    "n1r": {"squared": 1},
    "n2c": {"side_filled": 1, "logged": 1, "rstd": 1, "normed": 1},
    "n2r": {"side_filled": 1, "logged": 1, "rstd": 1, "normed": KC},
    "rt1": {"side_filled": 1, "rt_exp": 1, "routing": 19},
    "rt2": {"side_filled": 1, "comb_ready": 1},
    "z": {"side_filled": 1, "z_tanh": 1, "z_done": 1},
    "x_first": {"padded": 1, "side_filled": 1, "x_padded": 1, "conv": 2 * TAPS, "x_tanh": 1,
                "x_done": 1},
    "x": {"side_filled": 1, "x_padded": 1, "conv": 2 * TAPS, "x_tanh": 1, "x_done": 1},
    "split": {"side_filled": 1, "part_hi": 2, "part_rest": 1, "part_mid": 1, "part_lo": 1,
              "stacked": 16 * 4 * PARTS},
    "dt": {"side_filled": 1, "dt_pre": 4, "dt_exp": 1},
    "sp": {"dt_ln": 1, "dt_fix": 4, "dtx": 1, "y_init": JC, "decay_zero": 2},
    **{name: {"b_filled": 1, "c_filled": 1, "decay": 2, "driven": 1, "scanned": 1, "read_out": 1,
              "y_sum": sums} for name, sums in (("unit_first", 0), ("unit", 1), ("unit_last", 3))},
    "yz": {"y_gated": 1},
    "outp": {"side_filled": 1, "mixed": 2},
}
STARTS = {"x2_free": 16}


def kind_of(item):
    if item[0] == "n1":
        return "n1r" if item[1] in ("rms1", "rms2") else "n1c"
    if item[0] == "n2":
        return "n2r" if item[1] in ("rms1", "rms2") else "n2c"
    if item[0] in ("mg", "md", "mgn", "mdn"):
        return f"{item[0][:2]}{item[1] % MSLOTS}"
    if item == ("x", 0):
        return "x_first"
    if item[0] == "unit":
        return {0: "unit_first", PAIRS - 1: "unit_last"}.get(item[1] % PAIRS, "unit")
    return item[0]


def items_of(t):
    first, mamba, mlp, second = (0 <= t - lag < BATCH for lag in range(4))
    following = t + 1 < BATCH
    if t < 0:
        return [("load",), ("n1", "ln1"), ("n2", "ln1"), ("rt1", "f1")]
    hand = ([("hx", "f1")] if first else []) + ([("hx", "f2")] if second else [])
    hand += ([("rt2", "f1")] if first else []) + ([("rt2", "f2")] if second else [])
    keep = [("keep",)] if second else []
    keep += [("load",)] if following else []
    norms = [("n1", "lnA"), ("n2", "lnA"), ("n1", "rms1"), ("n2", "rms1")] if mamba else []
    project = ([("split", 0), ("x", 0), ("split", 1), ("x", 1), ("split", 2), ("z", 0), ("z", 1),
                ("dt", 0), ("dt", 1), ("sp",)] if mamba else [])
    units = [("unit", u) for u in range(UNITS)] if mamba else []
    last = [("yz",), ("outp",), ("n1", "rms2"), ("n2", "rms2")] if mamba else []
    r0 = ([("r0",)] if mamba else []) + ([("again",)] if first else [])
    ln2 = [("n1", "ln2"), ("n2", "ln2"), ("rt1", "f2")] if mlp else []
    ln1 = [("n1", "ln1"), ("n2", "ln1"), ("rt1", "f1")] if following else []
    ahead = [(k, c) for c in range(MSLOTS) for k in ("mgn", "mdn")] if 0 <= t + 1 - 2 < BATCH else []
    ff = ffn_items(first, second)
    along = norms + project
    scan = r0 + (merge(units, ln2 + ln1) if units else ln2 + ln1) + last
    if not mlp:
        return hand + keep + ahead + merge(ff[:-TAIL], along + scan) + ff[-TAIL:]
    if not mamba:
        return hand + keep + mlp_items() + ahead + merge(ff[:-TAIL], scan) + ff[-TAIL:]
    heavy = mlp_items() + ahead + ff[WSLOTS:]
    return hand + ff[:WSLOTS] + heavy[:6] + keep + merge(heavy[6:-TAIL], along + scan) + heavy[-TAIL:]


LENGTH = {"n1": 3, "n2": 5, "split": 5, "x": 5, "z": 3, "dt": 3, "sp": 8, "unit": 4, "rt1": 8,
          "yz": 2, "outp": 3, "g": 1.3, "u": 1.3, "down": 1.7, "gum": 1.7, "cmb": 0.2}
TAIL = 16


def merge(heavy, light):
    def starts(items):
        at, out = 0.0, []
        for it in items:
            out.append(at)
            at += LENGTH.get(it[0], 0.1)
        return [x / at for x in out]

    both = [(x, 0, i, it) for i, (x, it) in enumerate(zip(starts(heavy), heavy))]
    both += [(x, 1, i, it) for i, (x, it) in enumerate(zip(starts(light), light))]
    return [b[3] for b in sorted(both, key=lambda b: b[:3])]


def mlp_items():
    out = []
    for p in range(MLP_CHUNKS + 2):
        if p < MLP_CHUNKS:
            out.append(("gum", "mlp", p))
            if p + MSLOTS < MLP_CHUNKS:
                out.append(("mg", p + MSLOTS))
        if p >= 2:
            out.append(("down", "mlp", p - 2))
            if p - 2 + MSLOTS < MLP_CHUNKS:
                out.append(("md", p - 2 + MSLOTS))
    return out + [("end", "mlp")]


def ffn_items(first, second):
    if not (first or second):
        return []
    out = [("ws", c) for c in range(WSLOTS)]
    for p in range(FFN_CHUNKS + 2):
        now, before = p < FFN_CHUNKS, 1 <= p <= FFN_CHUNKS
        out += [("g", "ff", p)] if now else []
        out += [("cmb", "ff", p - 1)] if 1 <= p <= ROUTED else []
        out += [("by_u", "ff", p - 1)] if before else []
        out += [("down", "ff", p - 2)] if p >= 2 else []
        out += [("by_comb", "ff", p - 1)] if 1 <= p <= ROUTED else []
        out += [("u", "ff", p), ("by_g", "ff", p)] if now else []
        out += [("ws", p + WSLOTS)] if p + WSLOTS < FFN_CHUNKS else []
    return out + ([("end", "f1")] if first else []) + ([("end", "f2"), ("store",)] if second else [])


USES = {
    "side": {"n1c": [("centered", 1)], "n2c": [("logged", 1)], 
             "n2r": [("logged", 1)], "rt1": [("rt_exp", 1)], "rt2": [("comb_ready", 1)],
             "z": [("z_done", 1)], "x": [("x_padded", 1)],
             "x_first": [("x_padded", 1)], "split": [("part_rest", 1)],
             "dt": [("dt_pre", 4)], **{name: [("driven", 1), ("read_out", 1)] for name in ("unit_first", "unit", "unit_last")},
             "outp": [("mixed", 2)]},
    "gub": {"g": [("gated", 1)], "u": [("hidden", 1)], "gum": [("hidden", 1)]},
}
ENDED_BY = {"g": "by_g", "u": "by_u"}
BANKS = {"side": SIDES, "gub": GUBS}


class Ledger:

    def __init__(self, steps, turns, loop_at):
        self.steps, self.loop_at = steps, loop_at
        self.before, self.base = [], []
        self.uses = {pool: [] for pool in USES}
        self.use_base = {pool: [] for pool in USES}
        total, uses = dict(STARTS), dict.fromkeys(USES, 0)
        for n, items in enumerate(steps):
            self.base.append(dict(total))
            local, at, mine = {}, {}, {pool: [] for pool in USES}
            for it in items:
                assert it not in at, it
                at[it] = dict(local)
                for s, k in GROWS[kind_of(it)].items():
                    local[s] = local.get(s, 0) + k
                for pool, table in USES.items():
                    for w, (s, k) in enumerate(table.get(kind_of(it), [])):
                        mine[pool].append((it, w, s, k))
            self.before.append(at)
            times = turns if n == loop_at else 1
            for pool in USES:
                self.uses[pool].append(mine[pool])
                self.use_base[pool].append(uses[pool])
                uses[pool] += len(mine[pool]) * times
                assert n != loop_at or len(mine[pool]) % BANKS[pool] == 0, (pool, len(mine[pool]))
            if n == loop_at:
                self.per_turn = dict(local)
            for s, k in local.items():
                total[s] = total.get(s, 0) + k * times
        self.total = total


def macaron_kernel(nc, d):
    F32, F32R, BF16 = mybir.dt.float32, mybir.dt.float32r, mybir.dt.bfloat16
    ALU, ACT, AX = mybir.AluOpType, mybir.ActivationFunctionType, mybir.AxisListType

    times = [-1, 0, 1, 2, 3] + list(range(BATCH - 1, BATCH + 3))
    steps = [items_of(t) for t in times]
    LOOP = times.index(3)
    TURNS = BATCH - 1 - 3
    spans = [(0 if t < BATCH else SEQ, 2 * SEQ if t >= 3 else SEQ) for t in times]
    led = Ledger(steps, TURNS, LOOP)

    ctx = ExitStack()
    with ctx:
        def sb(name, shape, dt=F32):
            return ctx.enter_context(nc.sbuf_tensor(name, shape, dt))

        def bank(name):
            return ctx.enter_context(nc.psum_tensor(name, [P, 512], F32))

        w_gu = sb("w_gu", [P, FFN_CHUNKS, 2, KC, P])
        w_down = sb("w_down", [P, FFN_CHUNKS, DM])
        w_router = sb("w_router", [P, KC, EXPERTS])
        PROJ = 2 * DI + DI + DXB + RANK
        w_in = sb("w_in", [P, KC, PROJ])
        w_dt = sb("w_dt", [P, DI])
        w_out = sb("w_out", [P, JC, DM])
        vecs = sb("vecs", [P, JC, 3 + TAPS])
        lnw = sb("lnw", [P, 2, KC])
        a_neg = sb("a_neg", [P, JC, NST])
        mean_w = sb("mean_w", [P, P])
        eps_col = sb("eps_col", [P, 1])
        marks = sb("marks", [P, TT, 2])
        ident = sb("ident", [P, P], BF16)
        sel_e = sb("sel_e", [PARTS * EXPERTS, ROUTED * P], BF16)
        sel_b = sb("sel_b", [PARTS * 32, NST * P], BF16)
        sel_c = sb("sel_c", [PARTS * 32, 4 * P], BF16)
        xin = sb("xin", [P, KC, SEQ])
        x1 = sb("x1", [P, KC, SEQ])
        hn = sb("hn", [P, KC, SEQ])
        res = sb("res", [P, KC, SEQ])
        x2 = sb("x2", [P, KC, SEQ])
        x2kept = sb("x2kept", [P, KC, SEQ])
        xc = {"f1": sb("xc_f1", [P, KC, SEQ]),
              "f2": sb("xc_f2", [P, KC, SEQ])}
        x_hi = sb("x_hi", [P, KC, 2 * SEQ], F32R)
        x_lo = sb("x_lo", [P, KC, 2 * SEQ], F32R)
        xn_mlp = sb("xn_mlp", [P, KC, SEQ])
        comb = sb("comb", [PARTS * EXPERTS, 2 * SEQ], BF16)
        wr = [sb(f"wr{i}", [P, 2, 2, KC, P], F32R) for i in range(WSLOTS)]
        wm_gu = [sb(f"wm_gu{i}", [P, 2 * KC, P]) for i in range(MSLOTS)]
        wm_down = [sb(f"wm_down{i}", [P, KC, P]) for i in range(MSLOTS)]
        sq = sb("sq", [P, KC, SEQ])
        rstd = sb("rstd", [P, SEQ])
        hid = [sb(f"hid{i}", [P, 2 * SEQ]) for i in range(HSLOTS)]
        z2 = sb("z2", [P, JC, SEQ])
        xs = sb("xs", [P, JC, SEQ])
        dts = sb("dts", [P, JC, SEQ])
        dtx = sb("dtx", [P, JC, SEQ])
        y = xs
        rn = dts[:, 0:KC, :]
        bst = sb("bst", [PARTS * 32, JC, SEQ], BF16)
        cst = sb("cst", [PARTS * 32, 4, JC, SEQ], BF16)
        ring = sb("ring", [P, 4, 2, SEQ])
        ubuf = ring[:, :, :, :].rearrange("p a b s -> p (a b) s")[:, 0:JC, :]
        lbuf = ring[:, :, :, :].rearrange("p a b s -> p (a b) s")[:, JC:2 * JC, :]
        tmp = ring[:, 2, :, :]
        dtr = ring[:, 3, 1, :]
        ysum = ring[:, 3, :, :]
        xpad = ring[:, :, :, :].rearrange("p a b s -> p (a b s)")[
            :, 0:2 * (SEQ + TAPS - 1)].rearrange("p (h s) -> p h s", h=2)
        decays = sb("decays", [P, 2, 2, SEQ])
        decay = [decays[:, i, :, :] for i in range(2)]
        parts = decays[:, :, :, :].rearrange("p a h s -> p (a h s)").bitcast(BF16)[
            :, 0:PARTS * 2 * SEQ].rearrange("p (a h s) -> p a h s", a=PARTS, h=2)
        sc = sb("sc", [P, TT, SCW])
        rep = sb("rep", [P, TT, SCW])
        top8 = sb("top8", [P, TT, 8])
        e_sc = sb("e_sc", [P, TT, EXPERTS])
        cm = sb("cm", [P, TT, EXPERTS])
        pace = sb("pace", [P, 1])
        pool_pace = sb("pool_pace", [P, 1])
        csum = sb("csum", [P, TT])
        c3 = {call: sb(f"c3_{call}", [P, TT, PARTS * EXPERTS], BF16) for call in ("f1", "f2")}
        gub = [bank(f"gub{i}") for i in range(GUBS)]
        cmb = bank("cmb")
        acc = [bank(f"acc{i}") for i in range(KC)]
        side = [bank(f"side{i}") for i in range(SIDES)]

        names = sorted({s for g in GROWS.values() for s in g})
        sem = {s: ctx.enter_context(nc.semaphore(s)) for s in names}
        consts = ctx.enter_context(nc.semaphore("consts"))
        w_small = ctx.enter_context(nc.semaphore("w_small"))
        w_mamba = ctx.enter_context(nc.semaphore("w_mamba"))
        w_ffn = [ctx.enter_context(nc.semaphore(f"w_ffn{i}")) for i in range(4)]
        a_exp = ctx.enter_context(nc.semaphore("a_exp"))
        a_ready = ctx.enter_context(nc.semaphore("a_ready"))
        zeroed = ctx.enter_context(nc.semaphore("zeroed"))
        SLICES = [(0, 2), (2, 8), (8, 16), (16, FFN_CHUNKS)]

        block = ctx.enter_context(nc.Block())

        class Step:

            def __init__(self, eng, n, turn):
                self.eng, self.n, self.turn = eng, n, turn
                self.at = led.before[n]

            def t(self):
                return times[self.n] if self.turn is None else self.turn + times[self.n]

            def value(self, s, v):
                if self.turn is None:
                    return v if v > 0 else None
                assert v > 0, s
                return self.turn * led.per_turn.get(s, 0) + v

            def count(self, s, item, k, back=0):
                return self.value(s, led.base[self.n].get(s, 0) + self.at[item].get(s, 0) + k - back)

            def prior(self, s):
                v = led.base[self.n].get(s, 0)
                return self.value(s, v) if v else None

            def use(self, pool, item, w=0):
                mine = led.uses[pool][self.n]
                return led.use_base[pool][self.n] + next(
                    i for i, u in enumerate(mine) if u[0] == item and u[1] == w)

            def side_of(self, item, w=0):
                return side[self.use("side", item, w) % SIDES]

            def gub_of(self, item):
                return gub[self.use("gub", item) % GUBS]

            def last_use(self, pool, item, w=0):
                mine, back = led.uses[pool][self.n], BANKS[pool]
                local = self.use(pool, item, w) - led.use_base[pool][self.n]
                if local >= back:
                    it, _, s, k = mine[local - back]
                    it = (ENDED_BY.get(it[0], it[0]),) + it[1:]
                    return s, self.count(s, it, k)
                n = self.n - 1
                while n >= 0 and len(led.uses[pool][n]) < back:
                    n -= 1
                if n < 0:
                    return None
                s = led.uses[pool][n][local - back][2]
                assert self.n != LOOP or s == mine[local - back][2]
                return s, self.prior(s)

        def walk(eng, do):
            for n, items in enumerate(steps):
                if n == LOOP:
                    with eng.Fori(0, TURNS) as turn:
                        s = Step(eng, n, turn)
                        for it in items:
                            do(s, it)
                else:
                    s = Step(eng, n, None)
                    for it in items:
                        do(s, it)

        def pair(b):
            return b[:, :].rearrange("p (h s) -> p h s", h=2)

        def twice(ap):
            return ap.unsqueeze(1).broadcast_to([P, 2, SEQ])

        @block.sync
        def _(sp):
            for name, t in (("mean_w", mean_w), ("ident", ident), ("sel_e", sel_e),
                            ("sel_b", sel_b), ("sel_c", sel_c)):
                sp.dma_start(t[:], d[name]).then_inc(consts, 16)
            for name, t in (("w_router", w_router), ("vecs", vecs), ("lnw", lnw), ("a_log", a_neg)):
                sp.dma_start(t[:], d[name]).then_inc(w_small, 16)

            def ffn_slice(i):
                lo, hi = SLICES[i]
                sp.dma_start(w_gu[:, lo:hi], d["w_gu"][:, lo:hi]).then_inc(w_ffn[i], 16)
                sp.dma_start(w_down[:, lo:hi, :], d["w_down"][:, lo:hi, :]).then_inc(w_ffn[i], 16)

            def do(s, it):
                if it[0] == "load":
                    if (least := s.prior("centered")) is not None:
                        sp.wait_ge(sem["centered"], least)
                    sp.dma_start(xin[:], d["x"][s.t() + 1]).then_inc(sem["x_loaded"], 16)
                    if s.n == 0:
                        for i in range(4):
                            ffn_slice(i)
                        for name, t in (("w_in", w_in), ("w_dt", w_dt), ("w_out", w_out)):
                            sp.dma_start(t[:], d[name]).then_inc(w_mamba, 16)
                if it[0] == "split":
                    if it[1] == 0:
                        if (least := s.prior("c_filled")) is not None:
                            sp.wait_ge(sem["c_filled"], least)
                    sp.wait_ge(sem["part_lo"], s.count("part_lo", it, 1))
                    for q in range(4):
                        for a in range(PARTS):
                            rows = slice(32 * a, 32 * a + 32)
                            src = parts[32 * q:32 * q + 32, a, :, :]
                            if it[1] == 0:
                                dst, src = bst[rows, q, :], src[:, 0, :]
                            else:
                                j = 2 * (it[1] - 1)
                                dst = cst[rows, q, j:j + 2, :]
                            sp.dma_start(dst, src).then_inc(sem["stacked"], 16)
                if it[0] == "again":
                    if ("r0",) in s.at:
                        sp.wait_ge(sem["r_base"], s.count("r_base", ("r0",), 1))
                    sp.dma_start(x1[:], d["x"][s.t()]).then_inc(sem["x_again"], 16)
                if it[0] == "store":
                    sp.wait_ge(sem["residual"], s.count("residual", ("end", "f2"), KC))
                    sp.dma_start(d["out"][s.t() - 3], x2kept[:]).then_inc(sem["x2_free"], 16)

            walk(sp, do)
            sp.wait_ge(sem["x2_free"], STARTS["x2_free"] + 16 * BATCH)

        @block.tensor
        def _(pe):
            mm = nc.tensor.matmul
            pe.wait_ge(consts, 16 * 5)
            pe.wait_ge(w_small, 16 * 4)
            first_mamba = [True]

            def glu_half(s, it, half):
                c = it[2]
                a, b = spans[s.n]
                out = s.gub_of(it)[:, a:b]
                w = wr[c % WSLOTS]
                for k in range(KC):
                    mm(out, w[:, 0, half, k, :], x_hi[:, k, a:b], start=(k == 0), stop=False)
                    mm(out, w[:, 0, half, k, :], x_lo[:, k, a:b], start=False, stop=False)
                    last = mm(out, w[:, 1, half, k, :], x_hi[:, k, a:b], start=False,
                              stop=(k == KC - 1))
                return last

            def do(s, it):
                kind = it[0]
                if kind == "g":
                    c = it[2]
                    if c == 0:
                        for call in ("f1", "f2"):
                            if ("hx", call) in s.at:
                                pe.wait_ge(sem["x_split"], s.count("x_split", ("hx", call), 1))
                    pe.wait_ge(sem["w_split"], s.count("w_split", ("ws", c), 1))
                    if (over := s.last_use("gub", it)) is not None:
                        pe.wait_ge(sem[over[0]], over[1])
                    glu_half(s, it, 0).then_inc(sem["g_filled"], 1)
                elif kind == "u":
                    if (over := s.last_use("gub", it)) is not None:
                        pe.wait_ge(sem[over[0]], over[1])
                    glu_half(s, it, 1).then_inc(sem["u_filled"], 1)
                elif kind == "gum":
                    c = it[2]
                    if c == 0:
                        pe.wait_ge(sem["normed"], s.prior("normed"))
                    landed = f"mlp_gu{c % MSLOTS}"
                    if c < MSLOTS:
                        pe.wait_ge(sem[landed], s.prior(landed))
                    else:
                        pe.wait_ge(sem[landed], s.count(landed, ("mg", c), 16))
                    if (over := s.last_use("gub", it)) is not None:
                        pe.wait_ge(sem[over[0]], over[1])
                    b, w = s.gub_of(it), wm_gu[c % MSLOTS]
                    for half in range(2):
                        for k in range(KC):
                            last = mm(b[:, half * SEQ:(half + 1) * SEQ], w[:, half * KC + k, :],
                                      xn_mlp[:, k, :], start=(k == 0), stop=(k == KC - 1))
                    last.then_inc(sem["m_filled"], 1)
                elif kind == "cmb":
                    c = it[2]
                    a, b = spans[s.n]
                    if c == 0:
                        for call in ("f1", "f2"):
                            if ("rt2", call) in s.at:
                                pe.wait_ge(sem["comb_ready"], s.count("comb_ready", ("rt2", call), 1))
                    if (least := s.count("weighted", ("by_comb",) + it[1:], 1, back=1)) is not None:
                        pe.wait_ge(sem["weighted"], least)
                    mm(cmb[:, a:b], sel_e[:, c * P:(c + 1) * P], comb[:, a:b],
                       start=True, stop=True).then_inc(sem["comb_filled"], 1)
                elif kind == "down":
                    _, call, c = it
                    mlp = call == "mlp"
                    a, b = (0, SEQ) if mlp else spans[s.n]
                    if c == 0 and (least := s.count("residual", it, 0)) is not None:
                        pe.wait_ge(sem["residual"], least)
                    if not mlp and c < ROUTED:
                        pe.wait_ge(sem["weighted"], s.count("weighted", ("by_comb", call, c), 1))
                    else:
                        of = ("gum" if mlp else "by_u", call, c)
                        pe.wait_ge(sem["hidden"], s.count("hidden", of, 1))
                    if mlp:
                        landed = f"mlp_down{c % MSLOTS}"
                        if c < MSLOTS:
                            pe.wait_ge(sem[landed], s.prior(landed))
                        else:
                            pe.wait_ge(sem[landed], s.count(landed, ("md", c), 16))
                    h = hid[c % HSLOTS]
                    for k in range(KC):
                        w = wm_down[c % MSLOTS][:, k, :] if mlp else w_down[:, c, k * P:(k + 1) * P]
                        last = mm(acc[k][:, a:b], w, h[:, a:b], start=(c == 0),
                                  stop=(c == (MLP_CHUNKS if mlp else FFN_CHUNKS) - 1))
                    last.then_inc(sem["down_done"], 1)
                elif kind_of(it) == "n1c":
                    src = {"ln1": xin, "lnA": x1, "ln2": x2}[it[1]]
                    if it[1] == "ln1":
                        pe.wait_ge(sem["x_loaded"], s.count("x_loaded", ("load",), 16))
                    elif it[1] == "lnA":
                        if (least := s.prior("residual")) is not None:
                            pe.wait_ge(sem["residual"], least)
                    else:
                        pe.wait_ge(sem["residual"], s.count("residual", ("end", "mlp"), KC))
                    if (over := s.last_use("side", it)) is not None:
                        pe.wait_ge(sem[over[0]], over[1])
                    for k in range(KC):
                        last = mm(s.side_of(it)[:, 0:SEQ], mean_w[:], src[:, k, :],
                                  start=(k == 0), stop=(k == KC - 1))
                    last.then_inc(sem["side_filled"], 1)
                elif kind == "n2":
                    pe.wait_ge(sem["squared"], s.count("squared", ("n1", it[1]), 1))
                    if (over := s.last_use("side", it)) is not None:
                        pe.wait_ge(sem[over[0]], over[1])
                    for k in range(KC):
                        last = mm(s.side_of(it)[:, 0:SEQ], mean_w[:], sq[:, k, :],
                                  start=(k == 0), stop=(k == KC - 1))
                    last.then_inc(sem["side_filled"], 1)
                elif kind == "rt1":
                    norm = "ln1" if it[1] == "f1" else "ln2"
                    pe.wait_ge(sem["normed"], s.count("normed", ("n2", norm), 1))
                    if (over := s.last_use("side", it)) is not None:
                        pe.wait_ge(sem[over[0]], over[1])
                    b = s.side_of(it)
                    for tt in range(TT):
                        for k in range(KC):
                            last = mm(b[:, tt * EXPERTS:(tt + 1) * EXPERTS],
                                      xc[it[1]][:, k, tt * P:(tt + 1) * P], w_router[:, k, :],
                                      start=(k == 0), stop=(k == KC - 1))
                    last.then_inc(sem["side_filled"], 1)
                elif kind == "rt2":
                    pe.wait_ge(sem["routing"], s.prior("routing"))
                    if (over := s.last_use("side", it)) is not None:
                        pe.wait_ge(sem[over[0]], over[1])
                    b = s.side_of(it)[:, :].bitcast(BF16)
                    for tt in range(TT):
                        last = nc.tensor.transpose(b[0:PARTS * EXPERTS, tt * P:(tt + 1) * P],
                                                   c3[it[1]][:, tt, :], ident[:])
                    last.then_inc(sem["side_filled"], 1)
                elif kind in ("z", "x", "split"):
                    if kind == "split" and it[1] == 0:
                        pe.wait_ge(sem["normed"], s.count("normed", ("n2", "rms1"), KC))
                        if first_mamba[0]:
                            pe.wait_ge(w_mamba, 16 * 3)
                            first_mamba[0] = False
                    if (over := s.last_use("side", it)) is not None:
                        pe.wait_ge(sem[over[0]], over[1])
                    b = s.side_of(it)
                    at = {"z": 2 * it[1] * P, "x": DI + 2 * it[1] * P,
                          "split": 2 * DI + 2 * it[1] * P}[kind]
                    for h in range(2):
                        for k in range(KC):
                            last = mm(b[:, h * SEQ:(h + 1) * SEQ],
                                      w_in[:, k, at + h * P:at + (h + 1) * P], rn[:, k, :],
                                      start=(k == 0), stop=(k == KC - 1))
                    last.then_inc(sem["side_filled"], 1)
                elif kind == "dt":
                    pe.wait_ge(sem["part_hi"], s.count("part_hi", ("split", 0), 2))
                    if (over := s.last_use("side", it)) is not None:
                        pe.wait_ge(sem[over[0]], over[1])
                    b = s.side_of(it)
                    for h in range(2):
                        j = 2 * it[1] + h
                        last = mm(b[:, h * SEQ:(h + 1) * SEQ], w_dt[:, j * P:(j + 1) * P], dtr,
                                  start=True, stop=True)
                    last.then_inc(sem["side_filled"], 1)
                elif kind == "unit":
                    u = it[1]
                    j, p = u // PAIRS, u % PAIRS
                    if u == 0:
                        pe.wait_ge(sem["stacked"], s.count("stacked", ("split", 2), 16 * 4 * PARTS))
                    if (over := s.last_use("side", it, 0)) is not None:
                        pe.wait_ge(sem[over[0]], over[1])
                    b = s.side_of(it, 0)
                    for h in range(2):
                        n = 2 * p + h
                        last = mm(b[:, h * SEQ:(h + 1) * SEQ], sel_b[:, n * P:(n + 1) * P],
                                  bst[:, j, :], start=True, stop=True)
                    last.then_inc(sem["b_filled"], 1)
                    if (over := s.last_use("side", it, 1)) is not None:
                        pe.wait_ge(sem[over[0]], over[1])
                    b = s.side_of(it, 1)
                    for h in range(2):
                        n = 2 * p + h
                        last = mm(b[:, h * SEQ:(h + 1) * SEQ], sel_c[:, (n % 4) * P:(n % 4 + 1) * P],
                                  cst[:, n // 4, j, :], start=True, stop=True)
                    last.then_inc(sem["c_filled"], 1)
                elif kind == "outp":
                    pe.wait_ge(sem["y_gated"], s.count("y_gated", ("yz",), 1))
                    if (over := s.last_use("side", it)) is not None:
                        pe.wait_ge(sem[over[0]], over[1])
                    b = s.side_of(it)
                    for k in range(KC):
                        for j in range(JC):
                            last = mm(b[:, k * SEQ:(k + 1) * SEQ], w_out[:, j, k * P:(k + 1) * P],
                                      y[:, j, :], start=(j == 0), stop=(j == JC - 1))
                    last.then_inc(sem["side_filled"], 1)

            walk(pe, do)

        @block.scalar
        def _(act):
            A = nc.scalar.activation
            act.wait_ge(w_small, 16 * 4)
            A(a_neg[:], a_neg[:], ACT.Exp).then_inc(a_exp, 1)
            act.wait_ge(zeroed, 3)

            def do(s, it):
                kind = it[0]
                if kind == "ws":
                    c = it[1]
                    if s.n == 1:
                        for i, (lo, hi) in enumerate(SLICES):
                            if c == lo:
                                act.wait_ge(w_ffn[i], 32)
                    if c >= WSLOTS:
                        act.wait_ge(sem["u_filled"], s.count("u_filled", ("u", "ff", c - WSLOTS), 1))
                    elif (least := s.prior("u_filled")) is not None:
                        act.wait_ge(sem["u_filled"], least)
                    A(wr[c % WSLOTS][:, 0], w_gu[:, c], ACT.Copy).then_inc(sem["w_hi"], 1)
                elif kind in ("g", "gum"):
                    c = it[2]
                    a, b = (0, SEQ) if kind == "gum" else spans[s.n]
                    filled = "m_filled" if kind == "gum" else "g_filled"
                    act.wait_ge(sem[filled], s.count(filled, it, 1))
                    if (least := s.count("down_done", ("down",) + it[1:], 1,
                                         back=HSLOTS if c >= 2 else 2)) is not None:
                        act.wait_ge(sem["down_done"], least)
                    A(hid[c % HSLOTS][:, a:b], s.gub_of(it)[:, a:b], ACT.Tanh,
                      scale=0.5).then_inc(sem["tanh_done"], 1)
                elif kind == "n1":
                    src = {"ln1": xc["f1"], "ln2": xc["f2"]}.get(it[1], hn)
                    if kind_of(it) == "n1c":
                        act.wait_ge(sem["centered"], s.count("centered", it, 1))
                    elif it[1] == "rms1":
                        act.wait_ge(sem["normed"], s.count("normed", ("n2", "lnA"), 1))
                    else:
                        act.wait_ge(sem["mixed"], s.count("mixed", ("outp",), 1))
                    A(sq[:], src[:], ACT.Square).then_inc(sem["squared"], 1)
                elif kind == "n2":
                    act.wait_ge(sem["side_filled"], s.count("side_filled", it, 1))
                    A(rstd[:], s.side_of(it)[:, 0:SEQ], ACT.Ln,
                      bias=eps_col[:, 0:1]).then_inc(sem["logged"], 1)
                    act.wait_ge(sem["logged"], s.count("logged", it, 1))
                    A(rstd[:], rstd[:], ACT.Exp, scale=-0.5).then_inc(sem["rstd"], 1)
                elif kind == "rt1":
                    act.wait_ge(sem["side_filled"], s.count("side_filled", it, 1))
                    A(e_sc[:], s.side_of(it)[:, 0:TT * EXPERTS].rearrange("p (a e) -> p a e", a=TT),
                      ACT.Exp, scale=-1.0).then_inc(sem["rt_exp"], 1)
                elif kind == "z":
                    act.wait_ge(sem["side_filled"], s.count("side_filled", it, 1))
                    j = 2 * it[1]
                    if j == 0:
                        if (least := s.prior("y_gated")) is not None:
                            act.wait_ge(sem["y_gated"], least)
                    A(z2[:, j:j + 2, :], pair(s.side_of(it)), ACT.Tanh,
                      scale=0.5).then_inc(sem["z_tanh"], 1)
                elif kind == "x":
                    act.wait_ge(sem["side_filled"], s.count("side_filled", it, 1))
                    if it[1] == 0 and (least := s.prior("y_sum")) is not None:
                        act.wait_ge(sem["y_sum"], least)
                    if (least := s.count("conv", it, 0)) is not None:
                        act.wait_ge(sem["conv"], least)
                    A(xpad[:, :, TAPS - 1:], pair(s.side_of(it)), ACT.Copy).then_inc(sem["x_padded"], 1)
                    act.wait_ge(sem["conv"], s.count("conv", it, 2 * TAPS))
                    act.wait_ge(sem["part_lo"], s.count("part_lo", ("split", it[1]), 1))
                    if (least := s.count("x_done", it, 0)) is not None:
                        act.wait_ge(sem["x_done"], least)
                    A(tmp[:], xs[:, 2 * it[1]:2 * it[1] + 2, :], ACT.Tanh).then_inc(sem["x_tanh"], 1)
                elif kind == "split":
                    act.wait_ge(sem["side_filled"], s.count("side_filled", it, 1))
                    if it[1] == 0 and (least := s.prior("scanned")) is not None:
                        act.wait_ge(sem["scanned"], least)
                    if it[1] == 0 and (least := s.prior("y_sum")) is not None:
                        act.wait_ge(sem["y_sum"], least)
                    if (least := s.count("stacked", it, 0)) is not None:
                        act.wait_ge(sem["stacked"], least)
                    b = pair(s.side_of(it))
                    if it[1] == 0:
                        A(dtr, b[:, 1, :], ACT.Copy).then_inc(sem["part_hi"], 1)
                        A(parts[:, 0, 0, :], b[:, 0, :], ACT.Copy).then_inc(sem["part_hi"], 1)
                        act.wait_ge(sem["part_rest"], s.count("part_rest", it, 1))
                        A(parts[:, 1, 0, :], tmp[:, 0, :], ACT.Copy).then_inc(sem["part_mid"], 1)
                    else:
                        for h in range(2):
                            A(parts[:, 0, h, :], b[:, h, :], ACT.Copy).then_inc(sem["part_hi"], 1)
                        act.wait_ge(sem["part_rest"], s.count("part_rest", it, 1))
                        A(parts[:, 1, :, :], tmp[:], ACT.Copy).then_inc(sem["part_mid"], 1)
                elif kind == "dt":
                    act.wait_ge(sem["side_filled"], s.count("side_filled", it, 1))
                    if it[1] == 0:
                        act.wait_ge(sem["conv"], s.count("conv", ("x", 1), 2 * TAPS))
                        if (least := s.prior("y_sum")) is not None:
                            act.wait_ge(sem["y_sum"], least)
                        if (least := s.prior("decay")) is not None:
                            act.wait_ge(sem["decay"], least)
                    b = pair(s.side_of(it))
                    for h in range(2):
                        j = 2 * it[1] + h
                        A(ubuf[:, j, :], b[:, h, :], ACT.Abs, bias=vecs[:, j, 1:2]).then_inc(sem["dt_pre"], 1)
                        A(dts[:, j, :], b[:, h, :], ACT.Relu, bias=vecs[:, j, 1:2]).then_inc(sem["dt_pre"], 1)
                    act.wait_ge(sem["dt_pre"], s.count("dt_pre", it, 4))
                    u = ubuf[:, 2 * it[1]:2 * it[1] + 2, :]
                    A(u, u, ACT.Exp, scale=-1.0).then_inc(sem["dt_exp"], 1)
                elif kind == "sp":
                    act.wait_ge(sem["dt_exp"], s.count("dt_exp", ("dt", 1), 1))
                    act.wait_ge(sem["x_done"], s.count("x_done", ("x", 1), 1))
                    A(lbuf, ubuf, ACT.Ln, bias=1.0).then_inc(sem["dt_ln"], 1)
                elif kind == "unit":
                    u = it[1]
                    j, p = u // PAIRS, u % PAIRS
                    if u == 0:
                        act.wait_ge(sem["dt_fix"], s.count("dt_fix", ("sp",), 4))
                        if s.n == 2:
                            act.wait_ge(a_ready, 1)
                    if u < 2:
                        act.wait_ge(sem["stacked"], s.count("stacked", ("split", 2), 16 * 4 * PARTS))
                        act.wait_ge(sem["decay_zero"], s.count("decay_zero", ("sp",), 2))
                    if (least := s.count("scanned", it, 1, back=2)) is not None:
                        act.wait_ge(sem["scanned"], least)
                    for h in range(2):
                        n = 2 * p + h
                        A(decay[u % 2][:, h, 1:SEQ], dts[:, j, 1:SEQ], ACT.Exp,
                          scale=a_neg[:, j, n:n + 1]).then_inc(sem["decay"], 1)

            walk(act, do)

        @block.vector
        def _(dve):
            v = nc.vector
            v.memset(x2kept[:], 0.0).then_inc(sem["x2_free"], STARTS["x2_free"])
            v.memset(eps_col[:], EPS).then_inc(zeroed, 1)
            v.memset(marks[:, :, 0:1], -1.0).then_inc(zeroed, 1)
            v.memset(marks[:, :, 1:2], -2.0).then_inc(zeroed, 1)
            dve.wait_ge(zeroed, 3)
            dve.wait_ge(a_exp, 1)
            v.tensor_scalar(a_neg[:], a_neg[:], -1.0, None, ALU.mult).then_inc(a_ready, 1)
            v.tensor_copy(sc[:, :, EXPERTS:SCW], marks[:]).then_inc(a_ready, 1)
            v.tensor_scalar(vecs[:, :, 2:], vecs[:, :, 2:], 0.5, None, ALU.mult).then_inc(a_ready, 1)
            dve.wait_ge(a_ready, 3)

            def do(s, it):
                kind = it[0]
                if kind == "gum":
                    h, b = hid[it[2] % HSLOTS][:, 0:SEQ], s.gub_of(it)
                    dve.wait_ge(sem["tanh_done"], s.count("tanh_done", it, 1))
                    v.scalar_tensor_tensor(h, h, 1.0, b[:, 0:SEQ], ALU.add, ALU.mult).then_inc(sem["gated"], 1)
                    dve.wait_ge(sem["gated"], s.count("gated", it, 1))
                    v.tensor_tensor(h, h, b[:, SEQ:2 * SEQ], ALU.mult).then_inc(sem["hidden"], 1)
                elif kind in ("by_g", "by_u", "by_comb"):
                    c = it[2]
                    a, b = spans[s.n]
                    h = hid[c % HSLOTS][:, a:b]
                    if kind == "by_g":
                        of = ("g", "ff", c)
                        dve.wait_ge(sem["tanh_done"], s.count("tanh_done", of, 1))
                        v.scalar_tensor_tensor(h, h, 1.0, s.gub_of(of)[:, a:b], ALU.add,
                                               ALU.mult).then_inc(sem["gated"], 1)
                    elif kind == "by_u":
                        of = ("u", "ff", c)
                        dve.wait_ge(sem["gated"], s.count("gated", ("by_g", "ff", c), 1))
                        dve.wait_ge(sem["u_filled"], s.count("u_filled", of, 1))
                        v.tensor_tensor(h, h, s.gub_of(of)[:, a:b], ALU.mult).then_inc(sem["hidden"], 1)
                    else:
                        dve.wait_ge(sem["hidden"], s.count("hidden", ("by_u", "ff", c), 1))
                        dve.wait_ge(sem["comb_filled"], s.count("comb_filled", ("cmb", "ff", c), 1))
                        v.tensor_tensor(h, h, cmb[:, a:b], ALU.mult).then_inc(sem["weighted"], 1)
                elif kind == "end":
                    call = it[1]
                    last = ("down", "mlp", MLP_CHUNKS - 1) if call == "mlp" else ("down", "ff", FFN_CHUNKS - 1)
                    dve.wait_ge(sem["down_done"], s.count("down_done", last, 1))
                    a = SEQ if call == "f2" else 0
                    src, dst, scale = {"f1": (x1, x1, 0.25), "mlp": (res, x2, 0.5),
                                       "f2": (x2kept, x2kept, 0.25)}[call]
                    if call == "mlp" and ("keep",) in s.at:
                        dve.wait_ge(sem["kept"], s.count("kept", ("keep",), 1))
                    if call == "f1":
                        dve.wait_ge(sem["x_again"], s.count("x_again", ("again",), 16))
                    for k in range(KC):
                        v.scalar_tensor_tensor(dst[:, k, :], acc[k][:, a:a + SEQ], scale, src[:, k, :],
                                               ALU.mult, ALU.add).then_inc(sem["residual"], 1)
                elif kind == "hx":
                    src, a = xc[it[1]], 0 if it[1] == "f1" else SEQ
                    v.tensor_copy(x_hi[:, :, a:a + SEQ], src[:]).then_inc(sem["x_hi"], 1)
                    dve.wait_ge(sem["x_hi"], s.count("x_hi", it, 1))
                    v.tensor_tensor(x_lo[:, :, a:a + SEQ], src[:], x_hi[:, :, a:a + SEQ].bitcast(F32),
                                    ALU.subtract).then_inc(sem["x_split"], 1)
                elif kind == "keep":
                    dve.wait_ge(sem["x2_free"], s.prior("x2_free"))
                    v.tensor_copy(x2kept[:], x2[:]).then_inc(sem["kept"], 1)
                elif kind == "r0":
                    dve.wait_ge(sem["normed"], s.count("normed", ("n2", "lnA"), 1))
                    if ("end", "mlp") in s.at:
                        dve.wait_ge(sem["residual"], s.count("residual", ("end", "mlp"), KC))
                    v.tensor_tensor(res[:], x1[:], hn[:], ALU.add).then_inc(sem["r_base"], 1)
                elif kind == "n1":
                    if kind_of(it) == "n1c":
                        src, dst = {"ln1": (xin, xc["f1"]), "lnA": (x1, hn), "ln2": (x2, xc["f2"])}[it[1]]
                        dve.wait_ge(sem["side_filled"], s.count("side_filled", it, 1))
                        v.tensor_tensor(dst[:], src[:], twice(s.side_of(it)[:, 0:SEQ]),
                                        ALU.subtract).then_inc(sem["centered"], 1)
                elif kind == "n2":
                    dve.wait_ge(sem["rstd"], s.count("rstd", it, 1))
                    if it[1] in ("rms1", "rms2"):
                        dst = rn if it[1] == "rms1" else xn_mlp
                        i = 0 if it[1] == "rms1" else 1
                        if it[1] == "rms1" and (least := s.prior("decay")) is not None:
                            dve.wait_ge(sem["decay"], least)
                        for k in range(KC):
                            v.scalar_tensor_tensor(dst[:, k, :], hn[:, k, :], lnw[:, i, k:k + 1], rstd[:],
                                                   ALU.mult, ALU.mult).then_inc(sem["normed"], 1)
                    else:
                        dst = {"ln1": xc["f1"], "ln2": xc["f2"], "lnA": hn}[it[1]]
                        v.tensor_tensor(dst[:], dst[:], twice(rstd[:, :]), ALU.mult).then_inc(sem["normed"], 1)
                elif kind == "rt1":
                    route(s, it)
                elif kind == "rt2":
                    dve.wait_ge(sem["side_filled"], s.count("side_filled", it, 1))
                    a = 0 if it[1] == "f1" else SEQ
                    v.tensor_copy(comb[:, a:a + SEQ], s.side_of(it)[:, :].bitcast(BF16)[0:PARTS * EXPERTS, 0:SEQ]
                                  ).then_inc(sem["comb_ready"], 1)
                elif kind == "z":
                    j = 2 * it[1]
                    dve.wait_ge(sem["z_tanh"], s.count("z_tanh", it, 1))
                    v.scalar_tensor_tensor(z2[:, j:j + 2, :], z2[:, j:j + 2, :], 1.0, pair(s.side_of(it)),
                                           ALU.add, ALU.mult).then_inc(sem["z_done"], 1)
                elif kind == "x":
                    if it[1] == 0:
                        if (least := s.prior("y_sum")) is not None:
                            dve.wait_ge(sem["y_sum"], least)
                        v.memset(xpad[:, :, 0:TAPS - 1], 0.0).then_inc(sem["padded"], 1)
                        dve.wait_ge(sem["padded"], s.count("padded", it, 1))
                    dve.wait_ge(sem["x_padded"], s.count("x_padded", it, 1))
                    if it[1] == 0:
                        if (least := s.prior("y_init")) is not None:
                            dve.wait_ge(sem["y_init"], least)
                    for k in range(TAPS):
                        for h in range(2):
                            j = 2 * it[1] + h
                            o, i = xs[:, j, :], xpad[:, h, k:k + SEQ]
                            w = vecs[:, j, 3 + k:4 + k]
                            if k == 0:
                                v.tensor_scalar(o, i, w, vecs[:, j, 2:3], ALU.mult,
                                                ALU.add).then_inc(sem["conv"], 1)
                            else:
                                dve.wait_ge(sem["conv"], s.count("conv", it, 2 * k + h - 1))
                                v.scalar_tensor_tensor(o, i, w, o, ALU.mult,
                                                       ALU.add).then_inc(sem["conv"], 1)
                    dve.wait_ge(sem["x_tanh"], s.count("x_tanh", it, 1))
                    o = xs[:, 2 * it[1]:2 * it[1] + 2, :]
                    v.scalar_tensor_tensor(o, tmp[:], 1.0, o, ALU.add, ALU.mult).then_inc(sem["x_done"], 1)
                elif kind == "split":
                    if it[1] == 0 and (least := s.prior("y_sum")) is not None:
                        dve.wait_ge(sem["y_sum"], least)
                    dve.wait_ge(sem["part_hi"], s.count("part_hi", it, 2))
                    b = pair(s.side_of(it))
                    n = 1 if it[1] == 0 else 2
                    if (least := s.count("x_done", it, 0)) is not None:
                        dve.wait_ge(sem["x_done"], least)
                    v.tensor_tensor(tmp[:, 0:n, :], b[:, 0:n, :], parts[:, 0, 0:n, :],
                                    ALU.subtract).then_inc(sem["part_rest"], 1)
                    dve.wait_ge(sem["part_mid"], s.count("part_mid", it, 1))
                    v.tensor_tensor(parts[:, 2, 0:n, :], tmp[:, 0:n, :], parts[:, 1, 0:n, :],
                                    ALU.subtract).then_inc(sem["part_lo"], 1)
                elif kind == "sp":
                    dve.wait_ge(sem["stacked"], s.count("stacked", ("split", 2), 16 * 4 * PARTS))
                    for i in range(2):
                        v.memset(decay[i][:, :, 0:1], 0.0).then_inc(sem["decay_zero"], 1)
                    dve.wait_ge(sem["dt_exp"], s.count("dt_exp", ("dt", 1), 1))
                    if (least := s.prior("driven")) is not None:
                        dve.wait_ge(sem["driven"], least)
                    v.tensor_scalar(dtx[:], ubuf, 1.0, -1.0, ALU.add, ALU.add).then_inc(sem["dt_fix"], 1)
                    dve.wait_ge(sem["dt_fix"], s.count("dt_fix", it, 1))
                    v.tensor_tensor(dtx[:], ubuf, dtx[:], ALU.subtract).then_inc(sem["dt_fix"], 1)
                    dve.wait_ge(sem["dt_fix"], s.count("dt_fix", it, 2))
                    dve.wait_ge(sem["dt_ln"], s.count("dt_ln", it, 1))
                    v.tensor_tensor(dtx[:], dtx[:], lbuf, ALU.add).then_inc(sem["dt_fix"], 1)
                    dve.wait_ge(sem["dt_fix"], s.count("dt_fix", it, 3))
                    v.tensor_tensor(dts[:], dtx[:], dts[:], ALU.add).then_inc(sem["dt_fix"], 1)
                    dve.wait_ge(sem["dt_fix"], s.count("dt_fix", it, 4))
                    dve.wait_ge(sem["x_done"], s.count("x_done", ("x", 1), 1))
                    v.tensor_tensor(dtx[:], dts[:], xs[:], ALU.mult).then_inc(sem["dtx"], 1)
                    dve.wait_ge(sem["dtx"], s.count("dtx", it, 1))
                    for j in range(JC):
                        v.tensor_scalar(y[:, j, :], xs[:, j, :], vecs[:, j, 0:1], None,
                                        ALU.mult).then_inc(sem["y_init"], 1)
                elif kind == "unit":
                    u = it[1]
                    j = u // PAIRS
                    w = ring[:, u % 3, :, :]
                    if u == 0:
                        dve.wait_ge(sem["dtx"], s.count("dtx", ("sp",), 1))
                    if u >= 3:
                        by = u - 3 if (u - 3) % PAIRS else u - 2
                        dve.wait_ge(sem["y_sum"], s.count("y_sum", ("unit", by), 1))
                    dve.wait_ge(sem["b_filled"], s.count("b_filled", it, 1))
                    v.tensor_tensor(w, twice(dtx[:, j, :]), pair(s.side_of(it, 0)),
                                    ALU.mult).then_inc(sem["driven"], 1)
                    dve.wait_ge(sem["decay"], s.count("decay", it, 2))
                    dve.wait_ge(sem["driven"], s.count("driven", it, 1))
                    wf = w.rearrange("p h s -> p (h s)")
                    v.tensor_tensor_scan(wf, decay[u % 2][:, :, :].rearrange("p h s -> p (h s)"), wf,
                                         0.0, ALU.mult, ALU.add).then_inc(sem["scanned"], 1)
                    dve.wait_ge(sem["c_filled"], s.count("c_filled", it, 1))
                    dve.wait_ge(sem["scanned"], s.count("scanned", it, 1))
                    v.tensor_tensor(w, w, pair(s.side_of(it, 1)), ALU.mult).then_inc(sem["read_out"], 1)
                elif kind == "yz":
                    dve.wait_ge(sem["y_sum"], s.count("y_sum", ("unit", UNITS - 1), 3))
                    dve.wait_ge(sem["z_done"], s.count("z_done", ("z", 1), 1))
                    v.tensor_tensor(y[:], y[:], z2[:], ALU.mult).then_inc(sem["y_gated"], 1)
                elif kind == "outp":
                    dve.wait_ge(sem["side_filled"], s.count("side_filled", it, 1))
                    dve.wait_ge(sem["r_base"], s.count("r_base", ("r0",), 1))
                    b = pair(s.side_of(it))
                    v.scalar_tensor_tensor(hn[:], b, 0.5, hn[:], ALU.mult, ALU.add).then_inc(sem["mixed"], 1)
                    v.scalar_tensor_tensor(res[:], b, 0.5, res[:], ALU.mult, ALU.add).then_inc(sem["mixed"], 1)

            def route(s, it):
                done = [0]

                def link(ins):
                    done[0] += 1
                    ins.then_inc(sem["routing"], 1)

                def settle():
                    dve.wait_ge(sem["routing"], s.count("routing", it, done[0]))

                dve.wait_ge(sem["rt_exp"], s.count("rt_exp", it, 1))
                link(v.tensor_scalar(e_sc[:], e_sc[:], 1.0, None, ALU.add))
                settle()
                link(v.reciprocal(sc[:, :, 0:EXPERTS], e_sc[:]))
                settle()
                link(v.memset(pace[:], 0.0))
                for tt in range(TT):
                    link(v.max(top8[:, tt, :], sc[:, tt, 0:EXPERTS]))
                settle()
                link(v.tensor_copy(top8[:, :, TOPK:8], marks[:]))
                settle()
                link(v.memset(pace[:], 0.0))
                for tt in range(TT):
                    link(v.match_replace(rep[:, tt, :], top8[:, tt, :], sc[:, tt, :], 0.0))
                settle()
                link(v.tensor_tensor(cm[:], sc[:, :, 0:EXPERTS], rep[:, :, 0:EXPERTS], ALU.subtract))
                settle()
                link(v.tensor_reduce(csum[:], cm[:], axis=AX.X, op=ALU.add))
                settle()
                link(v.tensor_scalar(csum[:], csum[:], 1e-20, None, ALU.add))
                settle()
                link(v.reciprocal(csum[:], csum[:]))
                settle()
                for tt in range(TT):
                    link(v.tensor_scalar(cm[:, tt, :], cm[:, tt, :], csum[:, tt:tt + 1], None, ALU.mult))
                settle()
                E = EXPERTS
                out = c3[it[1]]
                link(v.tensor_copy(out[:, :, 0:E], cm[:]))
                settle()
                link(v.tensor_tensor(cm[:], cm[:], out[:, :, 0:E], ALU.subtract))
                settle()
                link(v.tensor_copy(out[:, :, E:2 * E], cm[:]))
                settle()
                link(v.tensor_tensor(out[:, :, 2 * E:3 * E], cm[:], out[:, :, E:2 * E], ALU.subtract))
                assert done[0] == 19

            walk(dve, do)

        @block.gpsimd
        def _(pool):
            def do(s, it):
                if it[0] in ("mg", "md", "mgn", "mdn"):
                    c, gu = it[1], it[0][1] == "g"
                    signal, user = ("m_filled", "gum") if gu else ("down_done", "down")
                    if it[0][-1] != "n":
                        pool.wait_ge(sem[signal], s.count(signal, (user, "mlp", c - MSLOTS), 1))
                    elif ("end", "mlp") in s.at:
                        pool.wait_ge(sem[signal], s.count(signal, (user, "mlp", MLP_CHUNKS - 1), 1))
                    if (least := s.count("load_paced", it, 0)) is not None:
                        pool.wait_ge(sem["load_paced"], least)
                    nc.gpsimd.tensor_tensor(pool_pace[:], eps_col[:], eps_col[:],
                                            ALU.add).then_inc(sem["load_paced"], 1)
                    if gu:
                        pool.dma_start(wm_gu[c % MSLOTS][:], d["w_mlp"][c, :, 0:2 * KC]).then_inc(
                            sem[f"mlp_gu{c % MSLOTS}"], 16)
                    else:
                        pool.dma_start(wm_down[c % MSLOTS][:], d["w_mlp"][c, :, 2 * KC:3 * KC]).then_inc(
                            sem[f"mlp_down{c % MSLOTS}"], 16)
                if it[0] == "ws":
                    w = wr[it[1] % WSLOTS]
                    pool.wait_ge(sem["w_hi"], s.count("w_hi", it, 1))
                    nc.gpsimd.tensor_tensor(w[:, 1], w_gu[:, it[1]], w[:, 0].bitcast(F32),
                                            ALU.subtract).then_inc(sem["w_split"], 1)
                if it[0] == "unit" and it[1] % PAIRS:
                    u = it[1]
                    j, p = u // PAIRS, u % PAIRS
                    TT_ = nc.gpsimd.tensor_tensor
                    pool.wait_ge(sem["read_out"], s.count("read_out", it, 1))
                    if p == 1:
                        if j:
                            pool.wait_ge(sem["y_sum"], s.count("y_sum", it, 0))
                        TT_(ysum, ring[:, (u - 1) % 3], ring[:, u % 3], ALU.add).then_inc(sem["y_sum"], 1)
                    else:
                        pool.wait_ge(sem["y_sum"], s.count("y_sum", it, 0))
                        TT_(ysum, ysum, ring[:, u % 3], ALU.add).then_inc(sem["y_sum"], 1)
                    if p == PAIRS - 1:
                        pool.wait_ge(sem["y_sum"], s.count("y_sum", it, 1))
                        TT_(ysum[:, 0], ysum[:, 0], ysum[:, 1], ALU.add).then_inc(sem["y_sum"], 1)
                        if j == 0:
                            pool.wait_ge(sem["y_init"], s.count("y_init", ("sp",), JC))
                        pool.wait_ge(sem["y_sum"], s.count("y_sum", it, 2))
                        TT_(y[:, j], y[:, j], ysum[:, 0], ALU.add).then_inc(sem["y_sum"], 1)

            walk(pool, do)


def kernel(**inputs):
    import numpy as np
    import concourse.bacc as bacc
    from concourse import mybir as _m
    from concourse.bass_utils import run_bass_kernel_spmd as run
    import ml_dtypes

    g = {k.removeprefix("L0_"): np.asarray(v) for k, v in inputs.items()}
    c = np.ascontiguousarray

    def feat(a):
        return c(a.reshape(a.shape[0] // P, P, a.shape[1]).transpose(1, 0, 2))

    x = g["attn_hidden_states"]
    xt = c(x.reshape(BATCH, SEQ, KC, P).transpose(0, 3, 2, 1))
    pad = FFN_CHUNKS * P - EXPERTS * FEXP - FSH

    def columns(experts, shared):
        w = np.concatenate([experts.transpose(1, 0, 2).reshape(DM, -1), shared,
                            np.zeros((DM, pad), np.float32)], axis=1)
        return w.reshape(KC, P, FFN_CHUNKS, P).transpose(1, 2, 0, 3)

    w_gu = np.stack([columns(g["ffn_wg"], g["ffn_sg"]), columns(g["ffn_wu"], g["ffn_su"])], axis=2)
    down = feat(np.concatenate([g["ffn_wd"].reshape(EXPERTS * FEXP, DM), g["ffn_sd"],
                                np.zeros((pad, DM), np.float32)]))

    def hidden_chunks(w):
        return w.reshape(MLP_CHUNKS, P, KC, P).transpose(0, 3, 2, 1)

    w_mlp = np.concatenate([hidden_chunks(g["attn_gate_w"]), hidden_chunks(g["attn_up_w"]),
                            g["attn_down_w"].T.reshape(MLP_CHUNKS, P, KC, P)], axis=2)
    win = g["attn_in_proj_w"]
    zr = np.arange(DI)
    heads = DXB // NST
    rep = DI // DXB
    ch = np.arange(DI)
    xr = DI + (ch // (rep * NST)) * NST + ch % NST
    br = DI + DXB + np.arange(DXB)
    dr = 2 * DXB + 2 * DI + np.arange(RANK)
    q, hd, n4 = np.meshgrid(np.arange(4), np.arange(heads), np.arange(4), indexing="ij")
    cr = np.concatenate([(DI + 2 * DXB + (8 * j + hd) * NST + 4 * q + n4).ravel() for j in range(JC)])
    order = np.concatenate([zr, xr, br, dr, cr])
    w_in = feat(c(win[order].T))
    vecs = np.concatenate([g["attn_D_param"][:, None], g["attn_dt_proj_b"][:, None],
                           g["attn_conv_b"][:, None], g["attn_conv_w"][:, 0, :]], axis=1)
    lnw = np.stack([g["attn_ln1_w"], g["attn_ln2_w"]])
    bf = ml_dtypes.bfloat16
    m = np.arange(P)
    k96 = np.arange(PARTS * 32)[:, None] % 32
    f = np.arange(ROUTED * P)[None, :]
    sel_e = (k96 == f // FEXP).astype(bf)
    sel_b = np.concatenate([(k96 == (m[None] // 64) * NST + n) for n in range(NST)], 1).astype(bf)
    sel_c = np.concatenate([(k96 == (m[None] // NST) * 4 + n) for n in range(4)], 1).astype(bf)
    arrays = {
        "x": xt, "w_gu": w_gu, "w_down": down, "w_mlp": w_mlp,
        "w_router": feat(g["ffn_gate_w"]), "w_in": w_in, "w_dt": c(g["attn_dt_proj_w"].T),
        "w_out": feat(c(g["attn_out_proj_w"].T)),
        "vecs": feat(vecs), "lnw": c(lnw.reshape(2, KC, P).transpose(2, 0, 1)),
        "a_log": feat(g["attn_A_log"]),
        "mean_w": np.full((P, P), 1.0 / DM, np.float32), "ident": np.eye(P).astype(bf),
        "sel_e": sel_e, "sel_b": sel_b, "sel_c": sel_c,
    }
    arrays = {k: c(v) for k, v in arrays.items()}
    nc = bacc.Bacc("TRN2", target_bir_lowering=False, num_devices=1)
    d = {k: nc.dram_tensor(f"in_{k}", v.shape, _m.dt.from_np(v.dtype), kind="ExternalInput").ap()
         for k, v in arrays.items()}
    d["out"] = nc.dram_tensor("out", xt.shape, _m.dt.float32, kind="ExternalOutput").ap()
    macaron_kernel(nc, d)
    r = run(nc, [{f"in_{k}": v for k, v in arrays.items()}], core_ids=[0])
    y = np.asarray(r.results[0]["out"])
    return c(y.transpose(0, 3, 2, 1)).reshape(BATCH, SEQ, DM)
```

```python
import concourse.bass as bass
from concourse import mybir
from contextlib import ExitStack

P = 128
SEQ, BATCH, DM = 256, 8, 256
KC = DM // P
EXPERTS, FEXP, TOPK, FSH = 32, 96, 6, 192
DI, NST, DXB, RANK, TAPS = 512, 16, 128, 128, 4
JC = DI // P
INTER = 1024
EPS = 1e-5
ROUTED = EXPERTS * FEXP // P
FFN_CHUNKS = ROUTED + -(-FSH // P)
MLP_CHUNKS = INTER // P
PARTS = 3
TT = SEQ // P
PAIRS = NST // 2
UNITS = JC * PAIRS
SCW = EXPERTS + 2
WSLOTS, MSLOTS, HSLOTS = 3, 3, 3
SIDES, GUBS = 2, 3

GROWS = {
    "load": {"x_loaded": 16},
    "store": {"x2_free": 16},
    **{f"mg{i}": {"load_paced": 1, f"mlp_gu{i}": 16} for i in range(MSLOTS)},
    **{f"md{i}": {"load_paced": 1, f"mlp_down{i}": 16} for i in range(MSLOTS)},
    "again": {"x_again": 16},
    "hx": {"x_hi": 1, "x_split": 1},
    "keep": {"kept": 1},
    "ws": {"w_hi": 1, "w_split": 1},
    "g": {"g_filled": 1, "tanh_done": 1},
    "by_g": {"gated": 1},
    "u": {"u_filled": 1},
    "by_u": {"hidden": 1},
    "gum": {"m_filled": 1, "tanh_done": 1, "gated": 1, "hidden": 1},
    "cmb": {"comb_filled": 1},
    "by_comb": {"weighted": 1},
    "down": {"down_done": 1},
    "end": {"residual": KC},
    "r0": {"r_base": 1},
    "n1c": {"side_filled": 1, "centered": 1, "squared": 1},
    "n1r": {"squared": 1},
    "n2c": {"side_filled": 1, "logged": 1, "rstd": 1, "normed": 1},
    "n2r": {"side_filled": 1, "logged": 1, "rstd": 1, "normed": KC},
    "rt1": {"side_filled": 1, "rt_exp": 1, "routing": 19},
    "rt2": {"side_filled": 1, "comb_ready": 1},
    "z": {"side_filled": 1, "z_tanh": 1, "z_done": 1},
    "x_first": {"padded": 1, "side_filled": 1, "x_padded": 1, "conv": 2 * TAPS, "x_tanh": 1,
                "x_done": 1},
    "x": {"side_filled": 1, "x_padded": 1, "conv": 2 * TAPS, "x_tanh": 1, "x_done": 1},
    "split": {"side_filled": 1, "part_hi": 2, "part_rest": 1, "part_mid": 1, "part_lo": 1,
              "stacked": 16 * 4 * PARTS},
    "dt": {"side_filled": 1, "dt_pre": 4, "dt_exp": 1},
    "sp": {"dt_ln": 1, "dt_fix": 2, "decay_zero": 2},
    "sp_dt": {"dt_fix": 2},
    "sp_x": {"dtx": 1},
    "y0": {"y_init": JC},
    "ub": {"b_filled": 1, "decay": 2, "driven": 1},
    **{name: {"c_filled": 1, "scanned": 1, "read_out": 1, "y_sum": sums}
       for name, sums in (("unit_first", 0), ("unit", 1), ("unit_last", 3))},
    "yz": {"y_gated": 1},
    "outp": {"side_filled": 1, "mixed": 2},
}
STARTS = {"x2_free": 16}


def kind_of(item):
    if item[0] == "n1":
        return "n1r" if item[1] in ("rms1", "rms2") else "n1c"
    if item[0] == "n2":
        return "n2r" if item[1] in ("rms1", "rms2") else "n2c"
    if item[0] in ("mg", "md", "mgn", "mdn"):
        return f"{item[0][:2]}{item[1] % MSLOTS}"
    if item == ("x", 0):
        return "x_first"
    if item[0] == "unit":
        return {0: "unit_first", PAIRS - 1: "unit_last"}.get(item[1] % PAIRS, "unit")
    return item[0]


def items_of(t):
    first, mamba, mlp, second = (0 <= t - lag < BATCH for lag in range(4))
    following = t + 1 < BATCH
    if t < 0:
        return [("load",), ("n1", "ln1"), ("n2", "ln1"), ("rt1", "f1")]
    hand = ([("hx", "f1")] if first else []) + ([("hx", "f2")] if second else [])
    hand += ([("rt2", "f1")] if first else []) + ([("rt2", "f2")] if second else [])
    keep = [("keep",)] if second else []
    keep += [("load",)] if following else []
    norms = [("n1", "lnA"), ("n2", "lnA"), ("n1", "rms1"), ("n2", "rms1")] if mamba else []
    project = ([("split", 0), ("x", 0), ("split", 1), ("x", 1), ("z", 0), ("split", 2), ("z", 1),
                ("dt", 0), ("dt", 1), ("sp",), ("sp_dt",), ("sp_x",), ("y0",)] if mamba else [])
    units = [(k, u) for u in range(UNITS) for k in ("ub", "unit")] if mamba else []
    last = [("yz",), ("outp",), ("n1", "rms2"), ("n2", "rms2")] if mamba else []
    r0 = ([("r0",)] if mamba else []) + ([("again",)] if first else [])
    ln2 = [("n1", "ln2"), ("n2", "ln2"), ("rt1", "f2")] if mlp else []
    ln1 = [("n1", "ln1"), ("n2", "ln1"), ("rt1", "f1")] if following else []
    ahead = [(k, c) for c in range(MSLOTS) for k in ("mgn", "mdn")] if 0 <= t + 1 - 2 < BATCH else []
    ff = ffn_items(first, second)
    along = norms + project
    length = LENGTH if first and second else SHORT
    scan = r0 + (merge(units, ln2 + ln1, length) if units else ln2 + ln1) + last
    if not mlp:
        return hand + keep + merge(ff[:-TAIL], along + scan, length) + ahead + ff[-TAIL:]
    if not mamba:
        return hand + keep + mlp_items() + ahead + merge(ff[:-TAIL], scan, length) + ff[-TAIL:]
    heavy = mlp_items() + ahead + ff[WSLOTS:]
    mixed = heavy[:6] + keep + merge(heavy[6:-TAIL], along + scan, length)
    return hand + ff[:WSLOTS] + mixed + heavy[-TAIL:]


LENGTH = {"n1": 3, "n2": 5, "split": 2.25, "x": 10.0, "z": 3,
          "dt": 3, "sp": 3, "sp_dt": 3, "sp_x": 2, "y0": 2,
          "ub": 2, "unit": 2, ("unit", UNITS - 1): 8, "rt1": 8,
          "yz": 3.9, "outp": 3, "g": 1.3, "u": 1.3, "down": 1.7, "gum": 1.7, "cmb": 0.2}
SHORT = {"n1": 3, "n2": 8.0, "split": 2.25, "x": 5, "z": 3,
          "dt": 3, "sp": 3, "sp_dt": 3, "sp_x": 2, "y0": 2,
          "ub": 2, "unit": 2, ("unit", UNITS - 1): 8, "rt1": 8,
          "yz": 3.9, "outp": 3, "g": 1.3, "u": 1.3, "down": 1.7, "gum": 1.7, "cmb": 0.2}
TAIL = 6


def merge(heavy, light, length):
    def starts(items):
        at, out = 0.0, []
        for it in items:
            out.append(at)
            at += length.get(it, length.get(it[0], 0.1))
        return [x / at for x in out]

    both = [(x, 0, i, it) for i, (x, it) in enumerate(zip(starts(heavy), heavy))]
    both += [(x, 1, i, it) for i, (x, it) in enumerate(zip(starts(light), light))]
    return [b[3] for b in sorted(both, key=lambda b: b[:3])]


def mlp_items():
    out = []
    for p in range(MLP_CHUNKS + 2):
        if p < MLP_CHUNKS:
            out.append(("gum", "mlp", p))
            if p + MSLOTS < MLP_CHUNKS:
                out.append(("mg", p + MSLOTS))
        if p >= 2:
            out.append(("down", "mlp", p - 2))
            if p - 2 + MSLOTS < MLP_CHUNKS:
                out.append(("md", p - 2 + MSLOTS))
    return out + [("end", "mlp")]


def ffn_items(first, second):
    if not (first or second):
        return []
    out = [("ws", c) for c in range(WSLOTS)]
    for p in range(FFN_CHUNKS + 2):
        now, before = p < FFN_CHUNKS, 1 <= p <= FFN_CHUNKS
        out += [("g", "ff", p)] if now else []
        out += [("by_u", "ff", p - 1)] if before else []
        out += [("down", "ff", p - 2)] if p >= 2 else []
        out += [("cmb", "ff", p - 1), ("by_comb", "ff", p - 1)] if 1 <= p <= ROUTED else []
        out += [("by_g", "ff", p), ("u", "ff", p)] if now else []
        out += [("ws", p + WSLOTS)] if p + WSLOTS < FFN_CHUNKS else []
    return out + ([("end", "f1")] if first else []) + ([("end", "f2"), ("store",)] if second else [])


LAG = {"n1": 0, "n2": 3, "split": 0, "x": 0, "z": 1, "dt": 0, "sp": 1, "sp_dt": 0,
       "sp_x": 0, "y0": 0, "ub": 0, "unit": 1, "rt1": 3, "outp": 4,
       "r0": 0, "yz": 0}
LATE = {"centered", "normed", "gated", "hidden", "weighted", "residual", "x_hi", "x_split", "kept",
        "r_base", "routing", "comb_ready", "z_done", "padded", "conv", "x_done", "part_rest",
        "part_lo", "dt_fix", "dtx", "y_init", "decay_zero", "driven", "scanned", "read_out",
        "y_gated", "mixed", "y_sum", "w_split", "load_paced"} | {
            f"mlp_{w}{i}" for w in ("gu", "down") for i in range(MSLOTS)}


def late_order(items):
    out, held, left = [], None, 0
    for it in items:
        light = it[0] in LAG
        if held is not None and (light or left == 0):
            out.append(held)
            held = None
        if light and LAG[it[0]]:
            held, left = it, LAG[it[0]]
        else:
            out.append(it)
            left -= 1
    return out + ([held] if held is not None else [])


USES = {
    "side": {"n1c": [("centered", 1)], "n2c": [("logged", 1)],
             "n2r": [("logged", 1)], "rt1": [("rt_exp", 1)], "rt2": [("comb_ready", 1)],
             "z": [("z_done", 1)], "x": [("x_padded", 1)],
             "x_first": [("x_padded", 1)], "split": [("part_rest", 1)],
             "dt": [("dt_pre", 4)], "ub": [("driven", 1)],
             **{name: [("read_out", 1)] for name in ("unit_first", "unit", "unit_last")},
             "outp": [("mixed", 2)]},
    "gub": {"g": [("gated", 1)], "u": [("hidden", 1)], "gum": [("hidden", 1)]},
}
ENDED_BY = {"g": "by_g", "u": "by_u"}
BANKS = {"side": SIDES, "gub": GUBS}


class Ledger:

    def __init__(self, steps, turns, loop_at):
        self.steps, self.loop_at = steps, loop_at
        self.before, self.base = [], []
        self.uses = {pool: [] for pool in USES}
        total = dict(STARTS)
        for n, items in enumerate(steps):
            self.base.append(dict(total))
            local, at, mine = {}, {it: {} for it in items}, {pool: [] for pool in USES}
            assert len(at) == len(items)
            for late, order in ((False, items), (True, late_order(items))):
                for it in order:
                    at[it].update({s: v for s, v in local.items() if (s in LATE) == late})
                    for s, k in GROWS[kind_of(it)].items():
                        if (s in LATE) == late:
                            local[s] = local.get(s, 0) + k
            for it in items:
                for pool, table in USES.items():
                    for w, (s, k) in enumerate(table.get(kind_of(it), [])):
                        mine[pool].append((it, w, s, k))
            self.before.append(at)
            times = turns if n == loop_at else 1
            for pool in USES:
                self.uses[pool].append(mine[pool])
            if n == loop_at:
                self.per_turn = dict(local)
            for s, k in local.items():
                total[s] = total.get(s, 0) + k * times
        self.total = total


def macaron_kernel(nc, d):
    F32, F32R, BF16 = mybir.dt.float32, mybir.dt.float32r, mybir.dt.bfloat16
    ALU, ACT, AX = mybir.AluOpType, mybir.ActivationFunctionType, mybir.AxisListType

    times = [-1, 0, 1, 2, 3] + list(range(BATCH - 1, BATCH + 3))
    steps = [items_of(t) for t in times]
    LOOP = times.index(3)
    TURNS = BATCH - 1 - 3
    spans = [(0 if t < BATCH else SEQ, 2 * SEQ if t >= 3 else SEQ) for t in times]
    led = Ledger(steps, TURNS, LOOP)

    ctx = ExitStack()
    with ctx:
        def sb(name, shape, dt=F32):
            return ctx.enter_context(nc.sbuf_tensor(name, shape, dt))

        def bank(name):
            return ctx.enter_context(nc.psum_tensor(name, [P, 512], F32))

        w_gu = sb("w_gu", [P, FFN_CHUNKS, 2, KC, P])
        w_down = sb("w_down", [P, FFN_CHUNKS, DM])
        w_router = sb("w_router", [P, KC, EXPERTS])
        PROJ = 2 * DI + DI + DXB + RANK
        w_in = sb("w_in", [P, KC, PROJ])
        w_dt = sb("w_dt", [P, DI])
        w_out = sb("w_out", [P, JC, DM])
        vecs = sb("vecs", [P, JC, 3 + TAPS])
        lnw = sb("lnw", [P, 2, KC])
        a_neg = sb("a_neg", [P, JC, NST])
        mean_w = sb("mean_w", [P, P])
        eps_col = sb("eps_col", [P, 1])
        marks = sb("marks", [P, TT, 2])
        ident = sb("ident", [P, P], BF16)
        sel_e = sb("sel_e", [PARTS * EXPERTS, ROUTED * P], BF16)
        sel_b = sb("sel_b", [PARTS * 32, NST * P], BF16)
        sel_c = sb("sel_c", [PARTS * 32, 4 * P], BF16)
        xin = sb("xin", [P, KC, SEQ])
        x1 = sb("x1", [P, KC, SEQ])
        hn = sb("hn", [P, KC, SEQ])
        res = sb("res", [P, KC, SEQ])
        x2 = sb("x2", [P, KC, SEQ])
        x2kept = sb("x2kept", [P, KC, SEQ])
        xc = {"f1": sb("xc_f1", [P, KC, SEQ]),
              "f2": sb("xc_f2", [P, KC, SEQ])}
        x_hi = sb("x_hi", [P, KC, 2 * SEQ], F32R)
        x_lo = sb("x_lo", [P, KC, 2 * SEQ], F32R)
        xn_mlp = sb("xn_mlp", [P, KC, SEQ])
        comb = sb("comb", [PARTS * EXPERTS, 2 * SEQ], BF16)
        wr = [sb(f"wr{i}", [P, 2, 2, KC, P], F32R) for i in range(WSLOTS)]
        wm_gu = [sb(f"wm_gu{i}", [P, 2 * KC, P]) for i in range(MSLOTS)]
        wm_down = [sb(f"wm_down{i}", [P, KC, P]) for i in range(MSLOTS)]
        sq = sb("sq", [P, KC, SEQ])
        rstd = sb("rstd", [P, SEQ])
        hid = [sb(f"hid{i}", [P, 2 * SEQ]) for i in range(HSLOTS)]
        z2 = sb("z2", [P, JC, SEQ])
        xs = sb("xs", [P, JC, SEQ])
        dts = sb("dts", [P, JC, SEQ])
        dtx = sb("dtx", [P, JC, SEQ])
        y = xs
        rn = dts[:, 0:KC, :]
        bst = sb("bst", [PARTS * 32, JC, SEQ], BF16)
        cst = sb("cst", [PARTS * 32, 4, JC, SEQ], BF16)
        ring = sb("ring", [P, 4, 2, SEQ])
        ubuf = ring[:, :, :, :].rearrange("p a b s -> p (a b) s")[:, 0:JC, :]
        lbuf = ring[:, :, :, :].rearrange("p a b s -> p (a b) s")[:, JC:2 * JC, :]
        tmp = ring[:, 2, :, :]
        dtr = ring[:, 3, 1, :]
        ysum = ring[:, 3, :, :]
        xpad = ring[:, :, :, :].rearrange("p a b s -> p (a b s)")[
            :, 0:2 * (SEQ + TAPS - 1)].rearrange("p (h s) -> p h s", h=2)
        decays = sb("decays", [P, 2, 2, SEQ])
        decay = [decays[:, i, :, :] for i in range(2)]
        parts = decays[:, :, :, :].rearrange("p a h s -> p (a h s)").bitcast(BF16)[
            :, 0:PARTS * 2 * SEQ].rearrange("p (a h s) -> p a h s", a=PARTS, h=2)
        sc = sb("sc", [P, TT, SCW])
        rep = sb("rep", [P, TT, SCW])
        top8 = sb("top8", [P, TT, 8])
        e_sc = sb("e_sc", [P, TT, EXPERTS])
        cm = sb("cm", [P, TT, EXPERTS])
        pace = sb("pace", [P, 1])
        pool_pace = sb("pool_pace", [P, 1])
        csum = sb("csum", [P, TT])
        c3 = {call: sb(f"c3_{call}", [P, TT, PARTS * EXPERTS], BF16) for call in ("f1", "f2")}
        gub = [bank(f"gub{i}") for i in range(GUBS)]
        cmb = bank("cmb")
        acc = [bank(f"acc{i}") for i in range(KC)]
        side = [bank(f"side{i}") for i in range(SIDES)]

        names = sorted({s for g in GROWS.values() for s in g})
        sem = {s: ctx.enter_context(nc.semaphore(s)) for s in names}
        w_mean = ctx.enter_context(nc.semaphore("w_mean"))
        consts = ctx.enter_context(nc.semaphore("consts"))
        w_small = ctx.enter_context(nc.semaphore("w_small"))
        w_mamba = ctx.enter_context(nc.semaphore("w_mamba"))
        w_ffn = [ctx.enter_context(nc.semaphore(f"w_ffn{i}")) for i in range(4)]
        a_exp = ctx.enter_context(nc.semaphore("a_exp"))
        a_ready = ctx.enter_context(nc.semaphore("a_ready"))
        zeroed = ctx.enter_context(nc.semaphore("zeroed"))
        SLICES = [(0, 2), (2, 8), (8, 16), (16, FFN_CHUNKS)]

        block = ctx.enter_context(nc.Block())

        class Step:

            def __init__(self, eng, n, turn):
                self.eng, self.n, self.turn = eng, n, turn
                self.at = led.before[n]

            def t(self):
                return times[self.n] if self.turn is None else self.turn + times[self.n]

            def value(self, s, v):
                if self.turn is None:
                    return v if v > 0 else None
                assert v > 0, s
                return self.turn * led.per_turn.get(s, 0) + v

            def count(self, s, item, k, back=0):
                return self.value(s, led.base[self.n].get(s, 0) + self.at[item].get(s, 0) + k - back)

            def prior(self, s):
                v = led.base[self.n].get(s, 0)
                return self.value(s, v) if v else None

            def use(self, pool, item, w=0):
                mine = led.uses[pool][self.n]
                return next(i for i, u in enumerate(mine) if u[0] == item and u[1] == w)

            def side_of(self, item, w=0):
                return side[self.use("side", item, w) % SIDES]

            def gub_of(self, item):
                return gub[self.use("gub", item) % GUBS]

            def last_use(self, pool, item, w=0):
                mine, back = led.uses[pool][self.n], BANKS[pool]
                local = self.use(pool, item, w)
                if local >= back:
                    it, _, s, k = mine[local - back]
                    it = (ENDED_BY.get(it[0], it[0]),) + it[1:]
                    return [(s, self.count(s, it, k))]
                ends = {u[2] for u in mine[-back:]} if self.n == LOOP else set()
                n = self.n - 1
                while n > 0 and len(led.uses[pool][n]) < back:
                    n -= 1
                ends |= {u[2] for u in led.uses[pool][n][-back:]} if n >= 0 else set()
                return [(s, self.prior(s)) for s in sorted(ends)]

        def walk(eng, do, late=False):
            for n, items in enumerate(steps):
                items = late_order(items) if late else items
                if n == LOOP:
                    with eng.Fori(0, TURNS) as turn:
                        s = Step(eng, n, turn)
                        for it in items:
                            do(s, it)
                else:
                    s = Step(eng, n, None)
                    for it in items:
                        do(s, it)

        def pair(b):
            return b[:, :].rearrange("p (h s) -> p h s", h=2)

        def twice(ap):
            return ap.unsqueeze(1).broadcast_to([P, 2, SEQ])

        @block.sync
        def _(sp):
            sp.dma_start(mean_w[:], d["mean_w"]).then_inc(w_mean, 16)

            def ffn_slice(i):
                lo, hi = SLICES[i]
                sp.dma_start(w_gu[:, lo:hi], d["w_gu"][:, lo:hi]).then_inc(w_ffn[i], 16)
                sp.dma_start(w_down[:, lo:hi, :], d["w_down"][:, lo:hi, :]).then_inc(w_ffn[i], 16)

            def do(s, it):
                if it[0] == "load":
                    if (least := s.prior("centered")) is not None:
                        sp.wait_ge(sem["centered"], least)
                    sp.dma_start(xin[:], d["x"][s.t() + 1]).then_inc(sem["x_loaded"], 16)
                    if s.n == 0:
                        for name, t in (("w_router", w_router), ("vecs", vecs), ("lnw", lnw),
                                        ("a_log", a_neg)):
                            sp.dma_start(t[:], d[name]).then_inc(w_small, 16)
                        ffn_slice(0)
                        for name, t in (("ident", ident), ("sel_e", sel_e), ("sel_b", sel_b),
                                        ("sel_c", sel_c)):
                            sp.dma_start(t[:], d[name]).then_inc(consts, 16)
                        ffn_slice(1)
                    if s.n == 1:
                        ffn_slice(2)
                        ffn_slice(3)
                        for name, t in (("w_in", w_in), ("w_dt", w_dt), ("w_out", w_out)):
                            sp.dma_start(t[:], d[name]).then_inc(w_mamba, 16)
                if it[0] == "split":
                    if it[1] == 0:
                        if (least := s.prior("c_filled")) is not None:
                            sp.wait_ge(sem["c_filled"], least)
                    sp.wait_ge(sem["part_lo"], s.count("part_lo", it, 1))
                    for q in range(4):
                        for a in range(PARTS):
                            rows = slice(32 * a, 32 * a + 32)
                            src = parts[32 * q:32 * q + 32, a, :, :]
                            if it[1] == 0:
                                dst, src = bst[rows, q, :], src[:, 0, :]
                            else:
                                j = 2 * (it[1] - 1)
                                dst = cst[rows, q, j:j + 2, :]
                            sp.dma_start(dst, src).then_inc(sem["stacked"], 16)
                if it[0] == "again":
                    if ("r0",) in s.at:
                        sp.wait_ge(sem["r_base"], s.count("r_base", ("r0",), 1))
                    sp.dma_start(x1[:], d["x"][s.t()]).then_inc(sem["x_again"], 16)
                if it[0] == "store":
                    sp.wait_ge(sem["residual"], s.count("residual", ("end", "f2"), KC))
                    sp.dma_start(d["out"][s.t() - 3], x2kept[:]).then_inc(sem["x2_free"], 16)

            walk(sp, do)
            sp.wait_ge(sem["x2_free"], STARTS["x2_free"] + 16 * BATCH)

        @block.tensor
        def _(pe):
            mm = nc.tensor.matmul
            pe.wait_ge(w_mean, 16)
            first_mamba = [True]

            def glu_half(s, it, half):
                c = it[2]
                a, b = spans[s.n]
                out = s.gub_of(it)[:, a:b]
                w = wr[c % WSLOTS]
                for k in range(KC):
                    mm(out, w[:, 0, half, k, :], x_hi[:, k, a:b], start=(k == 0), stop=False)
                    mm(out, w[:, 0, half, k, :], x_lo[:, k, a:b], start=False, stop=False)
                    last = mm(out, w[:, 1, half, k, :], x_hi[:, k, a:b], start=False,
                              stop=(k == KC - 1))
                return last

            def do(s, it):
                kind = it[0]
                if kind == "g":
                    c = it[2]
                    if c == 0:
                        for call in ("f1", "f2"):
                            if ("hx", call) in s.at:
                                pe.wait_ge(sem["x_split"], s.count("x_split", ("hx", call), 1))
                    pe.wait_ge(sem["w_split"], s.count("w_split", ("ws", c), 1))
                    for over, least in s.last_use("gub", it):
                        pe.wait_ge(sem[over], least)
                    glu_half(s, it, 0).then_inc(sem["g_filled"], 1)
                elif kind == "u":
                    for over, least in s.last_use("gub", it):
                        pe.wait_ge(sem[over], least)
                    glu_half(s, it, 1).then_inc(sem["u_filled"], 1)
                elif kind == "gum":
                    c = it[2]
                    if c == 0:
                        pe.wait_ge(sem["normed"], s.prior("normed"))
                    landed = f"mlp_gu{c % MSLOTS}"
                    if c < MSLOTS:
                        pe.wait_ge(sem[landed], s.prior(landed))
                    else:
                        pe.wait_ge(sem[landed], s.count(landed, ("mg", c), 16))
                    for over, least in s.last_use("gub", it):
                        pe.wait_ge(sem[over], least)
                    b, w = s.gub_of(it), wm_gu[c % MSLOTS]
                    for half in range(2):
                        for k in range(KC):
                            last = mm(b[:, half * SEQ:(half + 1) * SEQ], w[:, half * KC + k, :],
                                      xn_mlp[:, k, :], start=(k == 0), stop=(k == KC - 1))
                    last.then_inc(sem["m_filled"], 1)
                elif kind == "cmb":
                    c = it[2]
                    a, b = spans[s.n]
                    if c == 0:
                        for call in ("f1", "f2"):
                            if ("rt2", call) in s.at:
                                pe.wait_ge(sem["comb_ready"], s.count("comb_ready", ("rt2", call), 1))
                    if (least := s.count("weighted", ("by_comb",) + it[1:], 1, back=1)) is not None:
                        pe.wait_ge(sem["weighted"], least)
                    mm(cmb[:, a:b], sel_e[:, c * P:(c + 1) * P], comb[:, a:b],
                       start=True, stop=True).then_inc(sem["comb_filled"], 1)
                elif kind == "down":
                    _, call, c = it
                    mlp = call == "mlp"
                    a, b = (0, SEQ) if mlp else spans[s.n]
                    if c == 0 and (least := s.count("residual", it, 0)) is not None:
                        pe.wait_ge(sem["residual"], least)
                    if not mlp and c < ROUTED:
                        pe.wait_ge(sem["weighted"], s.count("weighted", ("by_comb", call, c), 1))
                    else:
                        of = ("gum" if mlp else "by_u", call, c)
                        pe.wait_ge(sem["hidden"], s.count("hidden", of, 1))
                    if mlp:
                        landed = f"mlp_down{c % MSLOTS}"
                        if c < MSLOTS:
                            pe.wait_ge(sem[landed], s.prior(landed))
                        else:
                            pe.wait_ge(sem[landed], s.count(landed, ("md", c), 16))
                    h = hid[c % HSLOTS]
                    for k in range(KC):
                        w = wm_down[c % MSLOTS][:, k, :] if mlp else w_down[:, c, k * P:(k + 1) * P]
                        last = mm(acc[k][:, a:b], w, h[:, a:b], start=(c == 0),
                                  stop=(c == (MLP_CHUNKS if mlp else FFN_CHUNKS) - 1))
                    last.then_inc(sem["down_done"], 1)
                elif kind_of(it) == "n1c":
                    src = {"ln1": xin, "lnA": x1, "ln2": x2}[it[1]]
                    if it[1] == "ln1":
                        pe.wait_ge(sem["x_loaded"], s.count("x_loaded", ("load",), 16))
                    elif it[1] == "lnA":
                        if (least := s.prior("residual")) is not None:
                            pe.wait_ge(sem["residual"], least)
                    else:
                        pe.wait_ge(sem["residual"], s.count("residual", ("end", "mlp"), KC))
                    for over, least in s.last_use("side", it):
                        pe.wait_ge(sem[over], least)
                    for k in range(KC):
                        last = mm(s.side_of(it)[:, 0:SEQ], mean_w[:], src[:, k, :],
                                  start=(k == 0), stop=(k == KC - 1))
                    last.then_inc(sem["side_filled"], 1)
                elif kind == "n2":
                    pe.wait_ge(sem["squared"], s.count("squared", ("n1", it[1]), 1))
                    for over, least in s.last_use("side", it):
                        pe.wait_ge(sem[over], least)
                    for k in range(KC):
                        last = mm(s.side_of(it)[:, 0:SEQ], mean_w[:], sq[:, k, :],
                                  start=(k == 0), stop=(k == KC - 1))
                    last.then_inc(sem["side_filled"], 1)
                elif kind == "rt1":
                    if s.n == 0:
                        pe.wait_ge(w_small, 16 * 4)
                    norm = "ln1" if it[1] == "f1" else "ln2"
                    pe.wait_ge(sem["normed"], s.count("normed", ("n2", norm), 1))
                    for over, least in s.last_use("side", it):
                        pe.wait_ge(sem[over], least)
                    b = s.side_of(it)
                    for tt in range(TT):
                        for k in range(KC):
                            last = mm(b[:, tt * EXPERTS:(tt + 1) * EXPERTS],
                                      xc[it[1]][:, k, tt * P:(tt + 1) * P], w_router[:, k, :],
                                      start=(k == 0), stop=(k == KC - 1))
                    last.then_inc(sem["side_filled"], 1)
                elif kind == "rt2":
                    if s.n == 1:
                        pe.wait_ge(consts, 16 * 4)
                    pe.wait_ge(sem["routing"], s.prior("routing"))
                    for over, least in s.last_use("side", it):
                        pe.wait_ge(sem[over], least)
                    b = s.side_of(it)[:, :].bitcast(BF16)
                    for tt in range(TT):
                        last = nc.tensor.transpose(b[0:PARTS * EXPERTS, tt * P:(tt + 1) * P],
                                                   c3[it[1]][:, tt, :], ident[:])
                    last.then_inc(sem["side_filled"], 1)
                elif kind in ("z", "x", "split"):
                    if kind == "split" and it[1] == 0:
                        pe.wait_ge(sem["normed"], s.count("normed", ("n2", "rms1"), KC))
                        if first_mamba[0]:
                            pe.wait_ge(w_mamba, 16 * 3)
                            first_mamba[0] = False
                    for over, least in s.last_use("side", it):
                        pe.wait_ge(sem[over], least)
                    b = s.side_of(it)
                    at = {"z": 2 * it[1] * P, "x": DI + 2 * it[1] * P,
                          "split": 2 * DI + 2 * it[1] * P}[kind]
                    for h in range(2):
                        for k in range(KC):
                            last = mm(b[:, h * SEQ:(h + 1) * SEQ],
                                      w_in[:, k, at + h * P:at + (h + 1) * P], rn[:, k, :],
                                      start=(k == 0), stop=(k == KC - 1))
                    last.then_inc(sem["side_filled"], 1)
                elif kind == "dt":
                    pe.wait_ge(sem["part_hi"], s.count("part_hi", ("split", 0), 2))
                    for over, least in s.last_use("side", it):
                        pe.wait_ge(sem[over], least)
                    b = s.side_of(it)
                    for h in range(2):
                        j = 2 * it[1] + h
                        last = mm(b[:, h * SEQ:(h + 1) * SEQ], w_dt[:, j * P:(j + 1) * P], dtr,
                                  start=True, stop=True)
                    last.then_inc(sem["side_filled"], 1)
                elif kind in ("ub", "unit"):
                    u = it[1]
                    j, p = u // PAIRS, u % PAIRS
                    if kind == "ub" and u == 0:
                        pe.wait_ge(sem["stacked"], s.count("stacked", ("split", 2), 16 * 4 * PARTS))
                    for over, least in s.last_use("side", it):
                        pe.wait_ge(sem[over], least)
                    b = s.side_of(it)
                    for h in range(2):
                        n = 2 * p + h
                        if kind == "ub":
                            last = mm(b[:, h * SEQ:(h + 1) * SEQ], sel_b[:, n * P:(n + 1) * P],
                                      bst[:, j, :], start=True, stop=True)
                        else:
                            last = mm(b[:, h * SEQ:(h + 1) * SEQ], sel_c[:, (n % 4) * P:(n % 4 + 1) * P],
                                      cst[:, n // 4, j, :], start=True, stop=True)
                    last.then_inc(sem["b_filled" if kind == "ub" else "c_filled"], 1)
                elif kind == "outp":
                    pe.wait_ge(sem["y_gated"], s.count("y_gated", ("yz",), 1))
                    for over, least in s.last_use("side", it):
                        pe.wait_ge(sem[over], least)
                    b = s.side_of(it)
                    for k in range(KC):
                        for j in range(JC):
                            last = mm(b[:, k * SEQ:(k + 1) * SEQ], w_out[:, j, k * P:(k + 1) * P],
                                      y[:, j, :], start=(j == 0), stop=(j == JC - 1))
                    last.then_inc(sem["side_filled"], 1)

            walk(pe, do)

        @block.scalar
        def _(act):
            A = nc.scalar.activation
            act.wait_ge(w_small, 16 * 4)
            A(a_neg[:], a_neg[:], ACT.Exp).then_inc(a_exp, 1)
            act.wait_ge(zeroed, 3)

            def do(s, it):
                kind = it[0]
                if kind == "ws":
                    c = it[1]
                    if s.n == 1:
                        for i, (lo, hi) in enumerate(SLICES):
                            if c == lo:
                                act.wait_ge(w_ffn[i], 32)
                    if c >= WSLOTS:
                        act.wait_ge(sem["u_filled"], s.count("u_filled", ("u", "ff", c - WSLOTS), 1))
                    elif (least := s.prior("u_filled")) is not None:
                        act.wait_ge(sem["u_filled"], least)
                    A(wr[c % WSLOTS][:, 0], w_gu[:, c], ACT.Copy).then_inc(sem["w_hi"], 1)
                elif kind in ("g", "gum"):
                    c = it[2]
                    a, b = (0, SEQ) if kind == "gum" else spans[s.n]
                    filled = "m_filled" if kind == "gum" else "g_filled"
                    act.wait_ge(sem[filled], s.count(filled, it, 1))
                    if (least := s.count("down_done", ("down",) + it[1:], 1,
                                         back=HSLOTS if c >= 2 else 2)) is not None:
                        act.wait_ge(sem["down_done"], least)
                    A(hid[c % HSLOTS][:, a:b], s.gub_of(it)[:, a:b], ACT.Tanh,
                      scale=0.5).then_inc(sem["tanh_done"], 1)
                elif kind == "n1":
                    src = {"ln1": xc["f1"], "ln2": xc["f2"]}.get(it[1], hn)
                    if kind_of(it) == "n1c":
                        act.wait_ge(sem["centered"], s.count("centered", it, 1))
                    elif it[1] == "rms1":
                        act.wait_ge(sem["normed"], s.count("normed", ("n2", "lnA"), 1))
                    else:
                        act.wait_ge(sem["mixed"], s.count("mixed", ("outp",), 1))
                    A(sq[:], src[:], ACT.Square).then_inc(sem["squared"], 1)
                elif kind == "n2":
                    act.wait_ge(sem["side_filled"], s.count("side_filled", it, 1))
                    A(rstd[:], s.side_of(it)[:, 0:SEQ], ACT.Ln,
                      bias=eps_col[:, 0:1]).then_inc(sem["logged"], 1)
                    act.wait_ge(sem["logged"], s.count("logged", it, 1))
                    A(rstd[:], rstd[:], ACT.Exp, scale=-0.5).then_inc(sem["rstd"], 1)
                elif kind == "rt1":
                    act.wait_ge(sem["side_filled"], s.count("side_filled", it, 1))
                    A(e_sc[:], s.side_of(it)[:, 0:TT * EXPERTS].rearrange("p (a e) -> p a e", a=TT),
                      ACT.Exp, scale=-1.0).then_inc(sem["rt_exp"], 1)
                elif kind == "z":
                    act.wait_ge(sem["side_filled"], s.count("side_filled", it, 1))
                    j = 2 * it[1]
                    if j == 0:
                        if (least := s.prior("y_gated")) is not None:
                            act.wait_ge(sem["y_gated"], least)
                    A(z2[:, j:j + 2, :], pair(s.side_of(it)), ACT.Tanh,
                      scale=0.5).then_inc(sem["z_tanh"], 1)
                elif kind == "x":
                    act.wait_ge(sem["side_filled"], s.count("side_filled", it, 1))
                    if it[1] == 0 and (least := s.prior("y_sum")) is not None:
                        act.wait_ge(sem["y_sum"], least)
                    if (least := s.count("conv", it, 0)) is not None:
                        act.wait_ge(sem["conv"], least)
                    A(xpad[:, :, TAPS - 1:], pair(s.side_of(it)), ACT.Copy).then_inc(sem["x_padded"], 1)
                    act.wait_ge(sem["conv"], s.count("conv", it, 2 * TAPS))
                    act.wait_ge(sem["part_lo"], s.count("part_lo", ("split", it[1]), 1))
                    if (least := s.count("x_done", it, 0)) is not None:
                        act.wait_ge(sem["x_done"], least)
                    A(tmp[:], xs[:, 2 * it[1]:2 * it[1] + 2, :], ACT.Tanh).then_inc(sem["x_tanh"], 1)
                elif kind == "split":
                    act.wait_ge(sem["side_filled"], s.count("side_filled", it, 1))
                    if it[1] == 0 and (least := s.prior("scanned")) is not None:
                        act.wait_ge(sem["scanned"], least)
                    if it[1] == 0 and (least := s.prior("y_sum")) is not None:
                        act.wait_ge(sem["y_sum"], least)
                    if (least := s.count("stacked", it, 0)) is not None:
                        act.wait_ge(sem["stacked"], least)
                    b = pair(s.side_of(it))
                    if it[1] == 0:
                        A(dtr, b[:, 1, :], ACT.Copy).then_inc(sem["part_hi"], 1)
                        A(parts[:, 0, 0, :], b[:, 0, :], ACT.Copy).then_inc(sem["part_hi"], 1)
                        act.wait_ge(sem["part_rest"], s.count("part_rest", it, 1))
                        A(parts[:, 1, 0, :], tmp[:, 0, :], ACT.Copy).then_inc(sem["part_mid"], 1)
                    else:
                        for h in range(2):
                            A(parts[:, 0, h, :], b[:, h, :], ACT.Copy).then_inc(sem["part_hi"], 1)
                        act.wait_ge(sem["part_rest"], s.count("part_rest", it, 1))
                        A(parts[:, 1, :, :], tmp[:], ACT.Copy).then_inc(sem["part_mid"], 1)
                elif kind == "dt":
                    act.wait_ge(sem["side_filled"], s.count("side_filled", it, 1))
                    if it[1] == 0:
                        act.wait_ge(sem["conv"], s.count("conv", ("x", 1), 2 * TAPS))
                        if (least := s.prior("y_sum")) is not None:
                            act.wait_ge(sem["y_sum"], least)
                        if (least := s.prior("decay")) is not None:
                            act.wait_ge(sem["decay"], least)
                    b = pair(s.side_of(it))
                    for h in range(2):
                        j = 2 * it[1] + h
                        A(ubuf[:, j, :], b[:, h, :], ACT.Abs, bias=vecs[:, j, 1:2]).then_inc(sem["dt_pre"], 1)
                        A(dts[:, j, :], b[:, h, :], ACT.Relu, bias=vecs[:, j, 1:2]).then_inc(sem["dt_pre"], 1)
                    act.wait_ge(sem["dt_pre"], s.count("dt_pre", it, 4))
                    u = ubuf[:, 2 * it[1]:2 * it[1] + 2, :]
                    A(u, u, ACT.Exp, scale=-1.0).then_inc(sem["dt_exp"], 1)
                elif kind == "sp":
                    act.wait_ge(sem["dt_exp"], s.count("dt_exp", ("dt", 1), 1))
                    act.wait_ge(sem["x_done"], s.count("x_done", ("x", 1), 1))
                    A(lbuf, ubuf, ACT.Ln, bias=1.0).then_inc(sem["dt_ln"], 1)
                elif kind == "ub":
                    u = it[1]
                    j, p = u // PAIRS, u % PAIRS
                    if u == 0:
                        act.wait_ge(sem["dt_fix"], s.count("dt_fix", ("sp_dt",), 2))
                        if s.n == 2:
                            act.wait_ge(a_ready, 1)
                    if u < 2:
                        act.wait_ge(sem["stacked"], s.count("stacked", ("split", 2), 16 * 4 * PARTS))
                        act.wait_ge(sem["decay_zero"], s.count("decay_zero", ("sp",), 2))
                    if (least := s.count("scanned", it, 1, back=2)) is not None:
                        act.wait_ge(sem["scanned"], least)
                    for h in range(2):
                        n = 2 * p + h
                        A(decay[u % 2][:, h, 1:SEQ], dts[:, j, 1:SEQ], ACT.Exp,
                          scale=a_neg[:, j, n:n + 1]).then_inc(sem["decay"], 1)

            walk(act, do)

        @block.vector
        def _(dve):
            v = nc.vector
            v.memset(x2kept[:], 0.0).then_inc(sem["x2_free"], STARTS["x2_free"])
            v.memset(eps_col[:], EPS).then_inc(zeroed, 1)
            v.memset(marks[:, :, 0:1], -1.0).then_inc(zeroed, 1)
            v.memset(marks[:, :, 1:2], -2.0).then_inc(zeroed, 1)
            dve.wait_ge(zeroed, 3)
            dve.wait_ge(a_exp, 1)
            v.tensor_scalar(a_neg[:], a_neg[:], -1.0, None, ALU.mult).then_inc(a_ready, 1)
            v.tensor_copy(sc[:, :, EXPERTS:SCW], marks[:]).then_inc(a_ready, 1)
            v.tensor_scalar(vecs[:, :, 2:], vecs[:, :, 2:], 0.5, None, ALU.mult).then_inc(a_ready, 1)
            dve.wait_ge(a_ready, 3)

            def do(s, it):
                kind = it[0]
                if kind == "gum":
                    h, b = hid[it[2] % HSLOTS][:, 0:SEQ], s.gub_of(it)
                    dve.wait_ge(sem["tanh_done"], s.count("tanh_done", it, 1))
                    v.scalar_tensor_tensor(h, h, 1.0, b[:, 0:SEQ], ALU.add, ALU.mult).then_inc(sem["gated"], 1)
                    dve.wait_ge(sem["gated"], s.count("gated", it, 1))
                    v.tensor_tensor(h, h, b[:, SEQ:2 * SEQ], ALU.mult).then_inc(sem["hidden"], 1)
                elif kind in ("by_g", "by_u", "by_comb"):
                    c = it[2]
                    a, b = spans[s.n]
                    h = hid[c % HSLOTS][:, a:b]
                    if kind == "by_g":
                        of = ("g", "ff", c)
                        dve.wait_ge(sem["tanh_done"], s.count("tanh_done", of, 1))
                        v.scalar_tensor_tensor(h, h, 1.0, s.gub_of(of)[:, a:b], ALU.add,
                                               ALU.mult).then_inc(sem["gated"], 1)
                    elif kind == "by_u":
                        of = ("u", "ff", c)
                        dve.wait_ge(sem["gated"], s.count("gated", ("by_g", "ff", c), 1))
                        dve.wait_ge(sem["u_filled"], s.count("u_filled", of, 1))
                        v.tensor_tensor(h, h, s.gub_of(of)[:, a:b], ALU.mult).then_inc(sem["hidden"], 1)
                    else:
                        dve.wait_ge(sem["hidden"], s.count("hidden", ("by_u", "ff", c), 1))
                        dve.wait_ge(sem["comb_filled"], s.count("comb_filled", ("cmb", "ff", c), 1))
                        v.tensor_tensor(h, h, cmb[:, a:b], ALU.mult).then_inc(sem["weighted"], 1)
                elif kind == "end":
                    call = it[1]
                    last = ("down", "mlp", MLP_CHUNKS - 1) if call == "mlp" else ("down", "ff", FFN_CHUNKS - 1)
                    dve.wait_ge(sem["down_done"], s.count("down_done", last, 1))
                    a = SEQ if call == "f2" else 0
                    src, dst, scale = {"f1": (x1, x1, 0.25), "mlp": (res, x2, 0.5),
                                       "f2": (x2kept, x2kept, 0.25)}[call]
                    if call == "mlp" and ("keep",) in s.at:
                        dve.wait_ge(sem["kept"], s.count("kept", ("keep",), 1))
                    if call == "f1":
                        dve.wait_ge(sem["x_again"], s.count("x_again", ("again",), 16))
                    for k in range(KC):
                        v.scalar_tensor_tensor(dst[:, k, :], acc[k][:, a:a + SEQ], scale, src[:, k, :],
                                               ALU.mult, ALU.add).then_inc(sem["residual"], 1)
                elif kind == "hx":
                    src, a = xc[it[1]], 0 if it[1] == "f1" else SEQ
                    v.tensor_copy(x_hi[:, :, a:a + SEQ], src[:]).then_inc(sem["x_hi"], 1)
                    dve.wait_ge(sem["x_hi"], s.count("x_hi", it, 1))
                    v.tensor_tensor(x_lo[:, :, a:a + SEQ], src[:], x_hi[:, :, a:a + SEQ].bitcast(F32),
                                    ALU.subtract).then_inc(sem["x_split"], 1)
                elif kind == "keep":
                    dve.wait_ge(sem["x2_free"], s.prior("x2_free"))
                    v.tensor_copy(x2kept[:], x2[:]).then_inc(sem["kept"], 1)
                elif kind == "r0":
                    dve.wait_ge(sem["normed"], s.count("normed", ("n2", "lnA"), 1))
                    if ("end", "mlp") in s.at:
                        dve.wait_ge(sem["residual"], s.count("residual", ("end", "mlp"), KC))
                    v.tensor_tensor(res[:], x1[:], hn[:], ALU.add).then_inc(sem["r_base"], 1)
                elif kind == "n1":
                    if kind_of(it) == "n1c":
                        src, dst = {"ln1": (xin, xc["f1"]), "lnA": (x1, hn), "ln2": (x2, xc["f2"])}[it[1]]
                        dve.wait_ge(sem["side_filled"], s.count("side_filled", it, 1))
                        v.tensor_tensor(dst[:], src[:], twice(s.side_of(it)[:, 0:SEQ]),
                                        ALU.subtract).then_inc(sem["centered"], 1)
                elif kind == "n2":
                    dve.wait_ge(sem["rstd"], s.count("rstd", it, 1))
                    if it[1] in ("rms1", "rms2"):
                        dst = rn if it[1] == "rms1" else xn_mlp
                        i = 0 if it[1] == "rms1" else 1
                        if it[1] == "rms1" and (least := s.prior("decay")) is not None:
                            dve.wait_ge(sem["decay"], least)
                        for k in range(KC):
                            v.scalar_tensor_tensor(dst[:, k, :], hn[:, k, :], lnw[:, i, k:k + 1], rstd[:],
                                                   ALU.mult, ALU.mult).then_inc(sem["normed"], 1)
                    else:
                        dst = {"ln1": xc["f1"], "ln2": xc["f2"], "lnA": hn}[it[1]]
                        v.tensor_tensor(dst[:], dst[:], twice(rstd[:, :]), ALU.mult).then_inc(sem["normed"], 1)
                elif kind == "rt1":
                    route(s, it)
                elif kind == "rt2":
                    dve.wait_ge(sem["side_filled"], s.count("side_filled", it, 1))
                    a = 0 if it[1] == "f1" else SEQ
                    v.tensor_copy(comb[:, a:a + SEQ], s.side_of(it)[:, :].bitcast(BF16)[0:PARTS * EXPERTS, 0:SEQ]
                                  ).then_inc(sem["comb_ready"], 1)
                elif kind == "z":
                    j = 2 * it[1]
                    dve.wait_ge(sem["z_tanh"], s.count("z_tanh", it, 1))
                    v.scalar_tensor_tensor(z2[:, j:j + 2, :], z2[:, j:j + 2, :], 1.0, pair(s.side_of(it)),
                                           ALU.add, ALU.mult).then_inc(sem["z_done"], 1)
                elif kind == "x":
                    if it[1] == 0:
                        if (least := s.prior("y_sum")) is not None:
                            dve.wait_ge(sem["y_sum"], least)
                        v.memset(xpad[:, :, 0:TAPS - 1], 0.0).then_inc(sem["padded"], 1)
                        dve.wait_ge(sem["padded"], s.count("padded", it, 1))
                    dve.wait_ge(sem["x_padded"], s.count("x_padded", it, 1))
                    if it[1] == 0:
                        if (least := s.prior("y_init")) is not None:
                            dve.wait_ge(sem["y_init"], least)
                    for k in range(TAPS):
                        for h in range(2):
                            j = 2 * it[1] + h
                            o, i = xs[:, j, :], xpad[:, h, k:k + SEQ]
                            w = vecs[:, j, 3 + k:4 + k]
                            if k == 0:
                                v.tensor_scalar(o, i, w, vecs[:, j, 2:3], ALU.mult,
                                                ALU.add).then_inc(sem["conv"], 1)
                            else:
                                dve.wait_ge(sem["conv"], s.count("conv", it, 2 * k + h - 1))
                                v.scalar_tensor_tensor(o, i, w, o, ALU.mult,
                                                       ALU.add).then_inc(sem["conv"], 1)
                    dve.wait_ge(sem["x_tanh"], s.count("x_tanh", it, 1))
                    o = xs[:, 2 * it[1]:2 * it[1] + 2, :]
                    v.scalar_tensor_tensor(o, tmp[:], 1.0, o, ALU.add, ALU.mult).then_inc(sem["x_done"], 1)
                elif kind == "split":
                    if it[1] == 0 and (least := s.prior("y_sum")) is not None:
                        dve.wait_ge(sem["y_sum"], least)
                    dve.wait_ge(sem["part_hi"], s.count("part_hi", it, 2))
                    b = pair(s.side_of(it))
                    n = 1 if it[1] == 0 else 2
                    if (least := s.count("x_done", it, 0)) is not None:
                        dve.wait_ge(sem["x_done"], least)
                    v.tensor_tensor(tmp[:, 0:n, :], b[:, 0:n, :], parts[:, 0, 0:n, :],
                                    ALU.subtract).then_inc(sem["part_rest"], 1)
                    dve.wait_ge(sem["part_mid"], s.count("part_mid", it, 1))
                    v.tensor_tensor(parts[:, 2, 0:n, :], tmp[:, 0:n, :], parts[:, 1, 0:n, :],
                                    ALU.subtract).then_inc(sem["part_lo"], 1)
                elif kind == "sp":
                    dve.wait_ge(sem["stacked"], s.count("stacked", ("split", 2), 16 * 4 * PARTS))
                    for i in range(2):
                        v.memset(decay[i][:, :, 0:1], 0.0).then_inc(sem["decay_zero"], 1)
                    dve.wait_ge(sem["dt_exp"], s.count("dt_exp", ("dt", 1), 1))
                    if (least := s.prior("driven")) is not None:
                        dve.wait_ge(sem["driven"], least)
                    v.tensor_scalar(dtx[:], ubuf, 1.0, -1.0, ALU.add, ALU.add).then_inc(sem["dt_fix"], 1)
                    dve.wait_ge(sem["dt_fix"], s.count("dt_fix", it, 1))
                    v.tensor_tensor(dtx[:], ubuf, dtx[:], ALU.subtract).then_inc(sem["dt_fix"], 1)
                elif kind == "sp_dt":
                    dve.wait_ge(sem["dt_fix"], s.count("dt_fix", ("sp",), 2))
                    dve.wait_ge(sem["dt_ln"], s.count("dt_ln", ("sp",), 1))
                    v.tensor_tensor(dtx[:], dtx[:], lbuf, ALU.add).then_inc(sem["dt_fix"], 1)
                    dve.wait_ge(sem["dt_fix"], s.count("dt_fix", it, 1))
                    v.tensor_tensor(dts[:], dtx[:], dts[:], ALU.add).then_inc(sem["dt_fix"], 1)
                elif kind == "sp_x":
                    dve.wait_ge(sem["dt_fix"], s.count("dt_fix", ("sp_dt",), 2))
                    dve.wait_ge(sem["x_done"], s.count("x_done", ("x", 1), 1))
                    v.tensor_tensor(dtx[:], dts[:], xs[:], ALU.mult).then_inc(sem["dtx"], 1)
                elif kind == "y0":
                    dve.wait_ge(sem["dtx"], s.count("dtx", ("sp_x",), 1))
                    for j in range(JC):
                        v.tensor_scalar(y[:, j, :], xs[:, j, :], vecs[:, j, 0:1], None,
                                        ALU.mult).then_inc(sem["y_init"], 1)
                elif kind == "ub":
                    u = it[1]
                    j = u // PAIRS
                    w = ring[:, u % 3, :, :]
                    if u == 0:
                        dve.wait_ge(sem["dtx"], s.count("dtx", ("sp_x",), 1))
                    if u >= 3:
                        by = u - 3 if (u - 3) % PAIRS else u - 2
                        dve.wait_ge(sem["y_sum"], s.count("y_sum", ("unit", by), 1))
                    dve.wait_ge(sem["b_filled"], s.count("b_filled", it, 1))
                    v.tensor_tensor(w, twice(dtx[:, j, :]), pair(s.side_of(it)),
                                    ALU.mult).then_inc(sem["driven"], 1)
                elif kind == "unit":
                    u = it[1]
                    w = ring[:, u % 3, :, :]
                    dve.wait_ge(sem["decay"], s.count("decay", ("ub", u), 2))
                    dve.wait_ge(sem["driven"], s.count("driven", ("ub", u), 1))
                    wf = w.rearrange("p h s -> p (h s)")
                    v.tensor_tensor_scan(wf, decay[u % 2][:, :, :].rearrange("p h s -> p (h s)"), wf,
                                         0.0, ALU.mult, ALU.add).then_inc(sem["scanned"], 1)
                    dve.wait_ge(sem["c_filled"], s.count("c_filled", it, 1))
                    dve.wait_ge(sem["scanned"], s.count("scanned", it, 1))
                    v.tensor_tensor(w, w, pair(s.side_of(it)), ALU.mult).then_inc(sem["read_out"], 1)
                elif kind == "yz":
                    dve.wait_ge(sem["y_sum"], s.count("y_sum", ("unit", UNITS - 1), 3))
                    dve.wait_ge(sem["z_done"], s.count("z_done", ("z", 1), 1))
                    v.tensor_tensor(y[:], y[:], z2[:], ALU.mult).then_inc(sem["y_gated"], 1)
                elif kind == "outp":
                    dve.wait_ge(sem["side_filled"], s.count("side_filled", it, 1))
                    dve.wait_ge(sem["r_base"], s.count("r_base", ("r0",), 1))
                    b = pair(s.side_of(it))
                    v.scalar_tensor_tensor(hn[:], b, 0.5, hn[:], ALU.mult, ALU.add).then_inc(sem["mixed"], 1)
                    v.scalar_tensor_tensor(res[:], b, 0.5, res[:], ALU.mult, ALU.add).then_inc(sem["mixed"], 1)

            def route(s, it):
                done = [0]

                def link(ins):
                    done[0] += 1
                    ins.then_inc(sem["routing"], 1)

                def settle():
                    dve.wait_ge(sem["routing"], s.count("routing", it, done[0]))

                dve.wait_ge(sem["rt_exp"], s.count("rt_exp", it, 1))
                link(v.tensor_scalar(e_sc[:], e_sc[:], 1.0, None, ALU.add))
                settle()
                link(v.reciprocal(sc[:, :, 0:EXPERTS], e_sc[:]))
                settle()
                link(v.memset(pace[:], 0.0))
                for tt in range(TT):
                    link(v.max(top8[:, tt, :], sc[:, tt, 0:EXPERTS]))
                settle()
                link(v.tensor_copy(top8[:, :, TOPK:8], marks[:]))
                settle()
                link(v.memset(pace[:], 0.0))
                for tt in range(TT):
                    link(v.match_replace(rep[:, tt, :], top8[:, tt, :], sc[:, tt, :], 0.0))
                settle()
                link(v.tensor_tensor(cm[:], sc[:, :, 0:EXPERTS], rep[:, :, 0:EXPERTS], ALU.subtract))
                settle()
                link(v.tensor_reduce(csum[:], cm[:], axis=AX.X, op=ALU.add))
                settle()
                link(v.tensor_scalar(csum[:], csum[:], 1e-20, None, ALU.add))
                settle()
                link(v.reciprocal(csum[:], csum[:]))
                settle()
                for tt in range(TT):
                    link(v.tensor_scalar(cm[:, tt, :], cm[:, tt, :], csum[:, tt:tt + 1], None, ALU.mult))
                settle()
                E = EXPERTS
                out = c3[it[1]]
                link(v.tensor_copy(out[:, :, 0:E], cm[:]))
                settle()
                link(v.tensor_tensor(cm[:], cm[:], out[:, :, 0:E], ALU.subtract))
                settle()
                link(v.tensor_copy(out[:, :, E:2 * E], cm[:]))
                settle()
                link(v.tensor_tensor(out[:, :, 2 * E:3 * E], cm[:], out[:, :, E:2 * E], ALU.subtract))
                assert done[0] == 19

            walk(dve, do, late=True)

        @block.gpsimd
        def _(pool):
            def do(s, it):
                if it[0] in ("mg", "md", "mgn", "mdn"):
                    c, gu = it[1], it[0][1] == "g"
                    signal, user = ("m_filled", "gum") if gu else ("down_done", "down")
                    if it[0][-1] != "n":
                        pool.wait_ge(sem[signal], s.count(signal, (user, "mlp", c - MSLOTS), 1))
                    elif ("end", "mlp") in s.at:
                        pool.wait_ge(sem[signal], s.count(signal, (user, "mlp", MLP_CHUNKS - 1), 1))
                    if (least := s.count("load_paced", it, 0)) is not None:
                        pool.wait_ge(sem["load_paced"], least)
                    nc.gpsimd.tensor_tensor(pool_pace[:], eps_col[:], eps_col[:],
                                            ALU.add).then_inc(sem["load_paced"], 1)
                    if gu:
                        pool.dma_start(wm_gu[c % MSLOTS][:], d["w_mlp"][c, :, 0:2 * KC]).then_inc(
                            sem[f"mlp_gu{c % MSLOTS}"], 16)
                    else:
                        pool.dma_start(wm_down[c % MSLOTS][:], d["w_mlp"][c, :, 2 * KC:3 * KC]).then_inc(
                            sem[f"mlp_down{c % MSLOTS}"], 16)
                if it[0] == "ws":
                    w = wr[it[1] % WSLOTS]
                    pool.wait_ge(sem["w_hi"], s.count("w_hi", it, 1))
                    nc.gpsimd.tensor_tensor(w[:, 1], w_gu[:, it[1]], w[:, 0].bitcast(F32),
                                            ALU.subtract).then_inc(sem["w_split"], 1)
                if it[0] == "unit" and it[1] % PAIRS:
                    u = it[1]
                    j, p = u // PAIRS, u % PAIRS
                    add = nc.gpsimd.tensor_tensor
                    pool.wait_ge(sem["read_out"], s.count("read_out", it, 1))
                    if p == 1:
                        if j:
                            pool.wait_ge(sem["y_sum"], s.count("y_sum", it, 0))
                        add(ysum, ring[:, (u - 1) % 3], ring[:, u % 3], ALU.add).then_inc(sem["y_sum"], 1)
                    else:
                        pool.wait_ge(sem["y_sum"], s.count("y_sum", it, 0))
                        add(ysum, ysum, ring[:, u % 3], ALU.add).then_inc(sem["y_sum"], 1)
                    if p == PAIRS - 1:
                        pool.wait_ge(sem["y_sum"], s.count("y_sum", it, 1))
                        add(ysum[:, 0], ysum[:, 0], ysum[:, 1], ALU.add).then_inc(sem["y_sum"], 1)
                        if j == 0:
                            pool.wait_ge(sem["y_init"], s.count("y_init", ("y0",), JC))
                        pool.wait_ge(sem["y_sum"], s.count("y_sum", it, 2))
                        add(y[:, j], y[:, j], ysum[:, 0], ALU.add).then_inc(sem["y_sum"], 1)

            walk(pool, do, late=True)


def kernel(**inputs):
    import numpy as np
    import concourse.bacc as bacc
    from concourse import mybir as _m
    from concourse.bass_utils import run_bass_kernel_spmd as run
    import ml_dtypes

    g = {k.removeprefix("L0_"): np.asarray(v) for k, v in inputs.items()}
    c = np.ascontiguousarray

    def feat(a):
        return c(a.reshape(a.shape[0] // P, P, a.shape[1]).transpose(1, 0, 2))

    x = g["attn_hidden_states"]
    xt = c(x.reshape(BATCH, SEQ, KC, P).transpose(0, 3, 2, 1))
    pad = FFN_CHUNKS * P - EXPERTS * FEXP - FSH

    def columns(experts, shared):
        w = np.concatenate([experts.transpose(1, 0, 2).reshape(DM, -1), shared,
                            np.zeros((DM, pad), np.float32)], axis=1)
        return w.reshape(KC, P, FFN_CHUNKS, P).transpose(1, 2, 0, 3)

    w_gu = np.stack([columns(g["ffn_wg"], g["ffn_sg"]), columns(g["ffn_wu"], g["ffn_su"])], axis=2)
    down = feat(np.concatenate([g["ffn_wd"].reshape(EXPERTS * FEXP, DM), g["ffn_sd"],
                                np.zeros((pad, DM), np.float32)]))

    def hidden_chunks(w):
        return w.reshape(MLP_CHUNKS, P, KC, P).transpose(0, 3, 2, 1)

    w_mlp = np.concatenate([hidden_chunks(g["attn_gate_w"]), hidden_chunks(g["attn_up_w"]),
                            g["attn_down_w"].T.reshape(MLP_CHUNKS, P, KC, P)], axis=2)
    win = g["attn_in_proj_w"]
    zr = np.arange(DI)
    heads = DXB // NST
    rep = DI // DXB
    ch = np.arange(DI)
    xr = DI + (ch // (rep * NST)) * NST + ch % NST
    br = DI + DXB + np.arange(DXB)
    dr = 2 * DXB + 2 * DI + np.arange(RANK)
    q, hd, n4 = np.meshgrid(np.arange(4), np.arange(heads), np.arange(4), indexing="ij")
    cr = np.concatenate([(DI + 2 * DXB + (8 * j + hd) * NST + 4 * q + n4).ravel() for j in range(JC)])
    order = np.concatenate([zr, xr, br, dr, cr])
    w_in = feat(c(win[order].T))
    vecs = np.concatenate([g["attn_D_param"][:, None], g["attn_dt_proj_b"][:, None],
                           g["attn_conv_b"][:, None], g["attn_conv_w"][:, 0, :]], axis=1)
    lnw = np.stack([g["attn_ln1_w"], g["attn_ln2_w"]])
    bf = ml_dtypes.bfloat16
    m = np.arange(P)
    k96 = np.arange(PARTS * 32)[:, None] % 32
    f = np.arange(ROUTED * P)[None, :]
    sel_e = (k96 == f // FEXP).astype(bf)
    sel_b = np.concatenate([(k96 == (m[None] // 64) * NST + n) for n in range(NST)], 1).astype(bf)
    sel_c = np.concatenate([(k96 == (m[None] // NST) * 4 + n) for n in range(4)], 1).astype(bf)
    arrays = {
        "x": xt, "w_gu": w_gu, "w_down": down, "w_mlp": w_mlp,
        "w_router": feat(g["ffn_gate_w"]), "w_in": w_in, "w_dt": c(g["attn_dt_proj_w"].T),
        "w_out": feat(c(g["attn_out_proj_w"].T)),
        "vecs": feat(vecs), "lnw": c(lnw.reshape(2, KC, P).transpose(2, 0, 1)),
        "a_log": feat(g["attn_A_log"]),
        "mean_w": np.full((P, P), 1.0 / DM, np.float32), "ident": np.eye(P).astype(bf),
        "sel_e": sel_e, "sel_b": sel_b, "sel_c": sel_c,
    }
    arrays = {k: c(v) for k, v in arrays.items()}
    nc = bacc.Bacc("TRN2", target_bir_lowering=False, num_devices=1)
    d = {k: nc.dram_tensor(f"in_{k}", v.shape, _m.dt.from_np(v.dtype), kind="ExternalInput").ap()
         for k, v in arrays.items()}
    d["out"] = nc.dram_tensor("out", xt.shape, _m.dt.float32, kind="ExternalOutput").ap()
    macaron_kernel(nc, d)
    r = run(nc, [{f"in_{k}": v for k, v in arrays.items()}], core_ids=[0])
    y = np.asarray(r.results[0]["out"])
    return c(y.transpose(0, 3, 2, 1)).reshape(BATCH, SEQ, DM)
```
